# Optimizing a Trainium2 kernel written in Bass

```python
import numpy as np
import jax
import jax.numpy as jnp

def _softmax(x, axis=-1):
    return jax.nn.softmax(x, axis=axis)

def _gelu(x):
    return jax.nn.gelu(x, approximate=True)

def _silu(x):
    return jax.nn.silu(x)

def _sigmoid(x):
    return jax.nn.sigmoid(x)

def _layernorm(x, axis=-1, eps=1e-05):
    m = jnp.mean(x, axis=axis, keepdims=True)
    v = jnp.var(x, axis=axis, keepdims=True)
    return (x - m) / jnp.sqrt(v + eps)

def _scatter_add(tgt, idx, src, axis=0):
    return tgt.at[idx].add(src)

def _segment_sum(src, seg, n):
    return jax.ops.segment_sum(src, seg, n)
kernel_name = 'mk_adj_ffn_d1_adj_r2_095170'

def setup_inputs(seed: int=0):
    np.random.seed(seed)
    _w = jnp.asarray

    def _rec_inputs():
        import jax
        import jax.numpy as jnp
        _gk = jax.random.key(seed)
        x = -0.0002928 + 1 * jax.random.normal(jax.random.fold_in(_gk, 1), (64, 128, 128), jnp.float32)
        _w = (1.0 + jnp.arange(128, dtype=jnp.float32)) ** (-0.5)
        _w = _w / _w.mean()
        _pij = jnp.clip(0.125 * _w[:, None] * _w[None, :], 0.0, 1.0)
        _a = jax.random.uniform(jax.random.fold_in(_gk, 2), (64, 128, 128)) < _pij
        adj = _a
        return (x, adj)
    x, adj = _rec_inputs()

    def _L0_gnn_setup():
        import jax, jax.numpy as jnp
        import numpy as np
        B, L, CIN, COUT, HEADS = (8, 1024, 128, 128, 4)
        HD = COUT // HEADS
        NEG_SLOPE = 0.2
        key = jax.random.key(seed)
        k1, k2, k3, k4, k5 = jax.random.split(key, 5)
        x = jax.random.normal(k1, (B, L, CIN), dtype=jnp.float32)
        adj_mask = jax.random.randint(k2, (B, L, L), 0, 2) > 0
        W = jax.random.normal(k3, (COUT, CIN), dtype=jnp.float32) * (1.0 / np.sqrt(CIN))
        att_src = jax.random.normal(k4, (1, HEADS, 1, HD), dtype=jnp.float32) * 0.1
        att_dst = jax.random.normal(k5, (1, HEADS, 1, HD), dtype=jnp.float32) * 0.1
        return {'x': x, 'adj_mask': adj_mask, 'W': W, 'att_src': att_src, 'att_dst': att_dst}
    _L0_gnn_all = _L0_gnn_setup()
    _L0_gnn_in = {k: v for k, v in _L0_gnn_all.items() if k in ('W', 'att_src', 'att_dst')}
    del _L0_gnn_all

    def _L0_ffn_setup():
        import jax, jax.numpy as jnp
        import numpy as np
        B, T, D, H, E = (16, 2048, 128, 256, 8)
        key = jax.random.key(seed)
        ks = jax.random.split(key, 5)
        x = jax.random.normal(ks[0], (B, T, D), dtype=jnp.float32)
        gate_w = jax.random.normal(ks[1], (D, E), dtype=jnp.float32) * 0.02
        gate_b = jnp.zeros((E,), dtype=jnp.float32)
        W1 = jax.random.normal(ks[2], (E, D, H), dtype=jnp.float32) * 0.02
        b1 = jnp.zeros((E, H), dtype=jnp.float32)
        W2 = jax.random.normal(ks[3], (E, H, D), dtype=jnp.float32) * 0.02
        b2 = jnp.zeros((E, D), dtype=jnp.float32)
        return {'x': x, 'gate_w': gate_w, 'gate_b': gate_b, 'W1': W1, 'b1': b1, 'W2': W2, 'b2': b2}
    _L0_ffn_all = _L0_ffn_setup()
    _L0_ffn_in = {k: v for k, v in _L0_ffn_all.items() if k in ('gate_w', 'gate_b', 'W1', 'b1', 'W2', 'b2')}
    del _L0_ffn_all
    return {'x': x, 'adj': adj, 'L0_gnn_W': _L0_gnn_in['W'], 'L0_gnn_att_src': _L0_gnn_in['att_src'], 'L0_gnn_att_dst': _L0_gnn_in['att_dst'], 'L0_ffn_gate_w': _L0_ffn_in['gate_w'], 'L0_ffn_gate_b': _L0_ffn_in['gate_b'], 'L0_ffn_W1': _L0_ffn_in['W1'], 'L0_ffn_b1': _L0_ffn_in['b1'], 'L0_ffn_W2': _L0_ffn_in['W2'], 'L0_ffn_b2': _L0_ffn_in['b2']}

def reference(x, adj, L0_gnn_W, L0_gnn_att_src, L0_gnn_att_dst, L0_ffn_gate_w, L0_ffn_gate_b, L0_ffn_W1, L0_ffn_b1, L0_ffn_W2, L0_ffn_b2):
    import jax
    import jax.numpy as jnp

    def _L0_gnn_ref(x, adj_mask, W, att_src, att_dst):
        import jax, jax.numpy as jnp
        import numpy as np
        B, L, CIN, COUT, HEADS = (8, 1024, 128, 128, 4)
        HD = COUT // HEADS
        NEG_SLOPE = 0.2
        Bb, Ll, _ = x.shape
        h = jnp.einsum('blc,oc->blo', x, W).reshape(Bb, Ll, HEADS, HD).transpose(0, 2, 1, 3)
        a_src = jnp.sum(h * att_src, axis=-1, keepdims=True)
        a_dst = jnp.sum(h * att_dst, axis=-1, keepdims=True)
        e = a_src + jnp.swapaxes(a_dst, 2, 3)
        e = jnp.where(e >= 0, e, NEG_SLOPE * e)
        fill = jnp.finfo(e.dtype).min
        e = jnp.where(adj_mask[:, None, :, :], e, fill)
        alpha = jax.nn.softmax(e, axis=-1)
        out = jnp.einsum('bhij,bhjd->bhid', alpha, h)
        return out.transpose(0, 2, 1, 3).reshape(Bb, Ll, COUT)

    def _L0_ffn_ref(x, gate_w, gate_b, W1, b1, W2, b2):
        import jax, jax.numpy as jnp
        import numpy as np
        B, T, D, H, E = (16, 2048, 128, 256, 8)
        Bb, Tt, Dd = x.shape
        Ee = gate_w.shape[1]
        xf = x.reshape(-1, Dd)
        N = xf.shape[0]
        logits = xf @ gate_w + gate_b
        probs = jax.nn.softmax(logits, axis=-1)
        top2_vals, top2_idx = jax.lax.top_k(probs, 2)
        cw = jnp.zeros((N, Ee), dtype=xf.dtype).at[jnp.arange(N)[:, None], top2_idx].add(top2_vals)

        def step(acc, params):
            w1, bb1, w2, bb2, we = params
            h = jax.nn.gelu(xf @ w1 + bb1, approximate=False)
            y = h @ w2 + bb2
            return (acc + we[:, None] * y, None)
        out, _ = jax.lax.scan(step, jnp.zeros_like(xf), (W1, b1, W2, b2, cw.T))
        return out.reshape(Bb, Tt, Dd)
    x = x + _L0_gnn_ref(_layernorm(x, axis=-1), adj, L0_gnn_W, L0_gnn_att_src, L0_gnn_att_dst)
    x = x + _L0_ffn_ref(_layernorm(x, axis=-1), L0_ffn_gate_w, L0_ffn_gate_b, L0_ffn_W1, L0_ffn_b1, L0_ffn_W2, L0_ffn_b2)
    return x

_drawn_inputs = setup_inputs


def setup_inputs(seed=0):
    import zlib

    import numpy as np

    out = dict(_drawn_inputs(seed))
    spreads = {'L0_ffn_gate_b': (0.0, 0.502), 'L0_ffn_b1': (0.0, 0.8), 'L0_ffn_b2': (0.0, 0.375)}
    factors = {'L0_ffn_gate_w': 2.868, 'L0_ffn_W1': 6.67, 'L0_ffn_W2': 6.067}
    for name, (base, spread) in spreads.items():
        noise = np.random.default_rng([zlib.crc32(name.encode()), seed]).standard_normal(out[name].shape)
        drawn = base * np.exp(spread * noise) if base else spread * noise
        out[name] = jnp.asarray(drawn.astype(out[name].dtype))
    for name, factor in factors.items():
        out[name] = (out[name] * factor).astype(out[name].dtype)
    return out
```

```python
import concourse.bass as bass
from concourse import mybir
from contextlib import ExitStack


def bass_gat_moe_kernel(nc, x, adj, w_rows, w_cols, att_src, att_dst, gate_w, gate_b, w1, b1, w2, b2,
                        pairs, out):
    f32, bf16 = mybir.dt.float32, mybir.dt.bfloat16
    u32, i32, u8 = mybir.dt.uint32, mybir.dt.int32, mybir.dt.uint8
    ALU, ACT, X = mybir.AluOpType, mybir.ActivationFunctionType, mybir.AxisListType.X

    P = 128
    G = 64
    T = 4
    GROUPS = G // T
    H, HD = 4, 32
    E = 8
    F = 256
    FC = F // P
    PAIRS = E * (E - 1) // 2
    N = G * P
    CAP = N + P
    DUMMY = PAIRS * CAP
    UNROLL = 4
    TILES = -(-((N + PAIRS * (P - 1)) // P) // UNROLL) * UNROLL
    EPS = 1e-5
    SLOPE = 0.2
    BIG = float(2.0 ** 100)
    NOWHERE = float(2 ** 20)
    CW, ID, RS, MEAN, ROW = P, P + E, P + E + 1, P + E + 2, P + E + 4
    W2C, B1C, B2C, EXP = F, F + FC * P, F + FC * P + FC, F + FC * P + FC + P // 2
    HW = P + 2 * H

    ctx = ExitStack()
    with ctx:
        def sb(name, shape, dt=f32):
            return ctx.enter_context(nc.sbuf_tensor(name, shape, dt))

        def sem(name):
            return ctx.enter_context(nc.semaphore(name))

        def sems(name, n):
            return [sem(f"{name}{i}") for i in range(n)]

        rows_dram = nc.dram_tensor("rows_by_pair", (DUMMY + P, ROW), f32, kind="Internal").ap()

        ident = sb("ident", [P, P])
        identb = sb("identb", [P, P], bf16)
        before = sb("before", [P, P], bf16)
        ones = sb("ones", [P, P], bf16)
        descend = sb("descend", [P, T, E])
        gbias = sb("gbias", [P, E])
        gw = sb("gw", [P, E])
        wu = sb("wu", [P, HW])
        w_raw = sb("w_raw", [P, P])
        att = sb("att", [P, 2 * H])
        experts = sb("experts", [P, E, EXP])
        b2w = sb("b2w", [3, 5, E * P])
        pair_ab = sb("pair_ab", [P, 2, PAIRS])
        pad = sb("pad", [P, ROW])
        x_all = sb("x_all", [P, G, P])
        adj_all = sb("adj_all", [P, G, P], u8)
        bn1 = sb("bn1", [P, T, 6])
        mv1 = sb("mv1", [P, T, 2])
        rs1 = sb("rs1", [P, T])
        xs = sb("xs", [P, T, P])
        var_eps = sb("var_eps", [P, T])
        minus_half = sb("minus_half", [P, T])
        xn = [sb(f"xn{i}", [P, T, P]) for i in range(2)]
        xnT = sb("xnT", [P, T, P])
        h = [sb(f"h{i}", [P, T, P]) for i in range(2)]
        sd = sb("sd", [P, 2, T * H])
        sd_rest = sb("sd_rest", [P, 2, 2, T * H])
        SIDE = T * P
        cols = [sb(f"cols{i}", [P, 2 * (SIDE + 3)], bf16) for i in range(2)]
        rows = [sb(f"rows{i}", [P, 2, T, P], bf16) for i in range(2)]
        mask = [sb(f"mask{i}", [P, T, P], bf16) for i in range(2)]
        nmax = [sb(f"nmax{i}", [P, T]) for i in range(2)]
        w = [sb(f"w{i}", [P, T, P]) for i in range(2)]
        z = [sb(f"z{i}", [P, T, P]) for i in range(2)]
        p = [sb(f"p{i}", [P, T, P]) for i in range(2)]
        pT = [sb(f"pT{i}", [P, T, P]) for i in range(2)]
        den = [sb(f"den{i}", [P, H, T]) for i in range(2)]
        rden = sb("rden", [P, H, T])
        oT = sb("oT", [P, T, P])
        outn = sb("outn", [P, T, P])
        R = [sb(f"R{i}", [P, T, ROW]) for i in range(2)]
        bn2 = sb("bn2", [P, T, 6])
        mv2 = sb("mv2", [P, T, 2])
        xs2 = sb("xs2", [P, T, P])
        xn2 = sb("xn2", [P, T, P])
        xn2T = sb("xn2T", [P, T, P])
        lg = sb("lg", [P, T, E])
        lmax = sb("lmax", [P, T])
        lsh = sb("lsh", [P, T, E])
        ex = sb("ex", [P, T, E])
        esum = sb("esum", [P, 2, T])
        prob = sb("prob", [P, T, E])
        best = sb("best", [P, T])
        tie = sb("tie", [P, 2, T, E])
        top = sb("top", [P, 3, T, E])
        left = sb("left", [P, T, E])
        member = sb("member", [P, T, PAIRS], bf16)
        run = sb("run", [P, T + 1, PAIRS])
        rank = sb("rank", [P, 2, T, PAIRS])
        slot = sb("slot", [P, T])
        slot_i = [sb(f"slot_i{i}", [P, T], u32) for i in range(2)]
        base = sb("base", [P, PAIRS])
        tiles = sb("tiles", [P, 12, PAIRS])
        tiles_i = sb("tiles_i", [P, 2, PAIRS], i32)
        number = sb("number", [P, 1])
        table = sb("table", [P, 4])
        table_i = sb("table_i", [4, P], i32)
        ends_i = sb("ends_i", [1, PAIRS], i32)
        XR = [sb(f"XR{i}", [P, ROW]) for i in range(UNROLL)]
        XN = [sb(f"XN{i}", [P, P]) for i in range(2)]
        XT = [sb(f"XT{i}", [P, P]) for i in range(2)]
        WS = [[sb(f"WS{i}{x_}", [P, EXP]) for x_ in range(2)] for i in range(2)]
        gT = [sb(f"gT{i}", [P, FC, P]) for i in range(2)]
        acc = [sb(f"acc{i}", [P, P]) for i in range(2)]
        Y = [sb(f"Y{i}", [P, P]) for i in range(UNROLL)]
        row_id = [sb(f"row_id{i}", [P, 1], u32) for i in range(UNROLL)]

        bank = [ctx.enter_context(nc.psum_tensor(f"bank{i}", [P, 512], f32)) for i in range(8)]
        e_ps, pT_ps, oT_ps = bank[0:2], bank[2:4], bank[4]
        five, six, seven = bank[5], bank[6], bank[7]

        const_made, weights_in, wu_ps, wu_made = sem("const_made"), sem("weights_in"), sem("wu_ps"), sem("wu_made")
        pool_const, pad_made = sem("pool_const"), sem("pad_made")
        b2_in, expert_in, b2_chain = sem("b2_in"), sem("expert_in"), sem("b2_chain")
        cols_set = sem("cols_set")
        x_in, adj_in = sems("x_in", 2), sems("adj_in", 2)
        ln1_made, xs_made, xn_made, xnT_done, xnT_made = map(sem, ("ln1_made", "xs_made", "xn_made", "xnT_done", "xnT_made"))
        h_done, h_made, sd_made, cols_made, rows_done = map(sem, ("h_done", "h_made", "sd_made", "cols_made", "rows_done"))
        rows_made, mask_made = sem("rows_made"), sem("mask_made")
        oT_made, out_done, outn_made, x2_made, ln2_made = map(sem, ("oT_made", "out_done", "outn_made", "x2_made", "ln2_made"))
        xs2_made, xn2_made, xn2T_done, xn2T_made, gate_done = map(sem, ("xs2_made", "xn2_made", "xn2T_done", "xn2T_made", "gate_done"))
        lsh_made, ex_made, member_made, rank_done, slot_made = map(sem, ("lsh_made", "ex_made", "member_made", "rank_done", "slot_made"))
        scattered = sems("scattered", 2)
        e_done, w_made, z_made, nmax_made, p_made, pT_done, pT_made, pv_done = map(
            sem, ("e_done", "w_made", "z_made", "nmax_made", "p_made", "pT_done", "pT_made", "pv_done"))
        c_ln1, c_split, c_norm, c_ln2, c_gate, c_top, c_slot, c_tiles, c_mean = map(
            sem, ("c_ln1", "c_split", "c_norm", "c_ln2", "c_gate", "c_top", "c_slot", "c_tiles", "c_mean"))
        table_done, table_made, pads_out = sem("table_done"), sem("table_made"), sem("pads_out")
        row_in = sems("row_in", UNROLL)
        xn_m, xT_done, xT_m, staged = sem("xn_m"), sem("xT_done"), sem("xT_m"), sem("staged")
        up_done, gelu_made, down_done, combined = sem("up_done"), sem("gelu_made"), sem("down_done"), sem("combined")
        ids_made = sem("ids_made")
        y_out = sems("y_out", UNROLL)

        stands_alone = sem("stands_alone")

        block = ctx.enter_context(nc.Block())

        class Chain:

            def __init__(self, eng, s, length):
                self.eng, self.s, self.length = eng, s, length

            def start(self, turn):
                self.turn, self.n = turn, 0

            def link(self, instruction):
                self.n += 1
                instruction.then_inc(self.s, 1)
                self.eng.wait_ge(self.s, self.turn * self.length + self.n)

            def end(self):
                assert self.n == self.length, (self.n, self.length)

        class At:

            def __init__(self, k, c):
                self.q, self.par, self.half, self.c = 2 * k + c, c % 2, k + c // 2, c
                self.static = isinstance(k, int)
                self.real = not self.static or 0 <= self.q < GROUPS
                self.second = not self.static or self.q >= 1
                self.third = not self.static or self.q >= 2

        def steps(eng, step):
            for c in range(-1, 4):
                step(0, c)
            with eng.Fori(2, GROUPS // 2 - 1) as k:
                step(k, 0)
                step(k, 1)
            for c in range(GROUPS - 2, GROUPS + 3):
                step(0, c)

        def unit(k, c, hd, back):
            i = hd - back
            return At(k, c - 1 + i // H), i % H

        def settle(eng):
            eng.sem_inc(stands_alone, 1)

        def xg(tensor, a):
            return tensor[:, bass.ds(a.q * T, T), :]

        @block.sync
        def _(sp):
            sp.dma_start(w_raw[:], w_rows).then_inc(weights_in, 16)
            sp.dma_start(wu[:, 0:P], w_cols).then_inc(weights_in, 16)
            sp.wait_ge(cols_set, 1)
            for hd in range(H):
                part = slice(hd * HD, (hd + 1) * HD)
                sp.dma_start(att[part, hd:hd + 1], att_src[hd, :].rearrange("(p a) -> p a", a=1)).then_inc(weights_in, 16)
                sp.dma_start(att[part, H + hd:H + hd + 1], att_dst[hd, :].rearrange("(p a) -> p a", a=1)).then_inc(weights_in, 16)
            for q in range(2):
                sp.dma_start(x_all[:, q * T:(q + 1) * T, :], x[:, q * T:(q + 1) * T, :]).then_inc(x_in[q], 16)
                sp.dma_start(adj_all[:, q * T:(q + 1) * T, :], adj[:, q * T:(q + 1) * T, :]).then_inc(adj_in[q], 16)
            sp.dma_start(gw[:], gate_w).then_inc(expert_in, 16)
            sp.dma_start(gbias[:], gate_b.partition_broadcast(P)).then_inc(expert_in, 16)
            sp.dma_start(pair_ab[:], pairs.partition_broadcast(P)).then_inc(expert_in, 16)
            sp.dma_start(b2w[:, 0, :], b2.partition_broadcast(3)).then_inc(b2_in, 16)
            sp.dma_start(experts[:, :, 0:F], w1).then_inc(expert_in, 16)
            sp.dma_start(experts[:, :, W2C:B1C], w2).then_inc(expert_in, 16)
            sp.dma_start(experts[:, :, B1C:B2C], b1).then_inc(expert_in, 16)
            with sp.Fori(1, GROUPS // 2) as k:
                for par in range(2):
                    at = bass.ds((2 * k + par) * T, T)
                    sp.wait_ge(x_in[par], 16 * k)
                    settle(sp)
                    sp.dma_start(x_all[:, at, :], x[:, at, :]).then_inc(x_in[par], 16)
                    sp.wait_ge(adj_in[par], 16 * k)
                    settle(sp)
                    sp.dma_start(adj_all[:, at, :], adj[:, at, :]).then_inc(adj_in[par], 16)

            sp.wait_ge(pad_made, 1)
            sp.dma_start(rows_dram[DUMMY:DUMMY + P, :], pad[:]).then_inc(pads_out, 16)
            sp.wait_ge(table_made, 1)
            BATCH = 7
            with sp.Fori(0, PAIRS // BATCH) as i:
                ends = [sp.value_load(ends_i[0:1, bass.ds(i * BATCH + j, 1)], min_val=0, max_val=DUMMY - P)
                        for j in range(BATCH)]
                for end in ends:
                    sp.dma_start(rows_dram[bass.ds(end, P), :], pad[:]).then_inc(pads_out, 16)
            for par in range(2):
                sp.wait_ge(scattered[par], 16 * T * GROUPS // 2)
            sp.wait_ge(pads_out, 16 * (PAIRS + 1))

            def fetch(n, j, value):
                sp.dma_start(XR[j][:], rows_dram[bass.ds(value, P), :]).then_inc(row_in[j], 16)

            def starts(n0):
                return [sp.value_load(table_i[0:1, bass.ds(n0 + j, 1)], min_val=0, max_val=DUMMY) for j in range(UNROLL)]

            for j, value in enumerate(starts(0)):
                fetch(j, j, value)
            with sp.Fori(1, TILES // UNROLL) as k:
                for j, value in enumerate(starts(k * UNROLL)):
                    sp.wait_ge(combined, 2 * ((k - 1) * UNROLL + j + 1))
                    sp.wait_ge(ids_made, (k - 1) * UNROLL + j + 1)
                    settle(sp)
                    fetch(k * UNROLL + j, j, value)
            for j in range(UNROLL):
                sp.wait_ge(y_out[j], 16 * (TILES // UNROLL))

        @block.gpsimd
        def _(pool):
            pool.memset(ident[:], 0.0).then_inc(pool_const, 1)
            pool.memset(ones[:], 1.0).then_inc(pool_const, 1)
            pool.memset(before[:], 1.0).then_inc(pool_const, 1)
            pool.wait_ge(pool_const, 3)
            pool.affine_select(out=ident[:], in_=ident[:], compare_op=ALU.not_equal, fill=1.0, base=0,
                               pattern=[[-1, P]], channel_multiplier=1).then_inc(pool_const, 1)
            pool.affine_select(out=before[:], in_=before[:], compare_op=ALU.is_gt, fill=0.0, base=0,
                               pattern=[[1, P]], channel_multiplier=-1).then_inc(pool_const, 1)
            pool.iota(descend[:], pattern=[[0, T], [-1, E]], base=E, channel_multiplier=0,
                      allow_small_or_imprecise_dtypes=True).then_inc(pool_const, 1)
            pool.iota(number[:], pattern=[[0, 1]], base=0, channel_multiplier=1,
                      allow_small_or_imprecise_dtypes=True).then_inc(pool_const, 1)
            pool.iota(base[:], pattern=[[CAP, PAIRS]], base=0, channel_multiplier=0,
                      allow_small_or_imprecise_dtypes=True).then_inc(pool_const, 1)
            pool.iota(run[:, 0, :], pattern=[[CAP, PAIRS]], base=0, channel_multiplier=0,
                      allow_small_or_imprecise_dtypes=True).then_inc(pool_const, 1)
            for par in range(2):
                pool.memset(R[par][:], 0.0).then_inc(pool_const, 1)
            pool.memset(pad[:], 0.0).then_inc(pool_const, 1)
            pool.memset(minus_half[:], -0.5).then_inc(pool_const, 1)
            pool.wait_ge(pool_const, 13)
            for par in range(2):
                pool.iota(R[par][:, :, ID], pattern=[[P, T]], base=(par - 2) * T * P, channel_multiplier=1,
                          allow_small_or_imprecise_dtypes=True).then_inc(const_made, 1)
            pool.memset(pad[:, ID:ID + 1], NOWHERE).then_inc(pad_made, 1)
            pool.tensor_copy(identb[:], ident[:]).then_inc(const_made, 1)

            def normalize(dst, mid, src, mv, rstd, mid_made, a):
                over = lambda v: v.unsqueeze(2).broadcast_to([P, T, P])
                settle(pool)
                pool.tensor_scalar(var_eps[:], mv[:, :, 1], EPS, None, ALU.add).then_inc(mid_made, 1)
                pool.tensor_tensor(mid[:], src, over(mv[:, :, 0]), ALU.subtract).then_inc(mid_made, 1)
                pool.wait_ge(mid_made, 3 * a.q + 2)
                pool.tensor_tensor(rstd, var_eps[:], minus_half[:], ALU.pow).then_inc(mid_made, 1)
                pool.wait_ge(mid_made, 3 * (a.q + 1))
                return pool.tensor_tensor(dst[:], mid[:], over(rstd), ALU.mult)

            def step(k, c):
                f, b, r = At(k, c + 1), At(k, c - 2), At(k, c - 3)
                if f.real:
                    pool.wait_ge(ln1_made, f.q + 1)
                    if f.third:
                        pool.wait_ge(xnT_done, f.q - 1)
                    normalize(xn[f.par], xs, xg(x_all, f), mv1, rs1[:], xs_made, f).then_inc(xn_made, 1)
                if b.real:
                    pool.wait_ge(outn_made, b.q + 1)
                    if b.third:
                        pool.wait_ge(scattered[b.par], 16 * T * b.half)
                    pool.tensor_tensor(R[b.par][:, :, 0:P], outn[:], xg(x_all, b), ALU.add).then_inc(x2_made, 1)
                    pool.wait_ge(ln2_made, b.q + 1)
                    if b.second:
                        pool.wait_ge(xn2T_done, b.q)
                    normalize(xn2, xs2, R[b.par][:, :, 0:P], mv2, R[b.par][:, :, RS], xs2_made, b).then_inc(xn2_made, 1)
                if r.real:
                    pool.wait_ge(slot_made, r.q + 1)
                    settle(pool)
                    for t in range(T):
                        pool.indirect_dma_start(
                            rows_dram, bass.IndirectOffsetOnAxis(ap=slot_i[r.par][:, t:t + 1], axis=0),
                            R[r.par][:, t, :], None).then_inc(scattered[r.par], 16)

            steps(pool, step)

            def place(k, j, first):
                n = k * UNROLL + j
                pool.wait_ge(row_in[j], 16 * (k + 1))
                if not first:
                    pool.wait_ge(y_out[j], 16 * k)
                settle(pool)
                pool.tensor_copy(row_id[j][:], XR[j][:, ID:ID + 1]).then_inc(ids_made, 1)
                pool.wait_ge(ids_made, n + 1)
                pool.wait_ge(combined, 2 * (n + 1))
                settle(pool)
                pool.indirect_dma_start(out, bass.IndirectOffsetOnAxis(ap=row_id[j][:], axis=0), Y[j][:], None,
                                        bounds_check=N - 1, oob_is_err=False).then_inc(y_out[j], 16)

            for j in range(UNROLL):
                place(0, j, True)
            with pool.Fori(1, TILES // UNROLL) as k:
                for j in range(UNROLL):
                    place(k, j, False)

        @block.scalar
        def _(act):
            def copy(dst, src):
                return act.activation(dst, src, ACT.Copy)

            def relu_unit(k, c, hd):
                a, hd = unit(k, c, hd, 0)
                if not a.real:
                    return
                u = a.q * H + hd
                act.wait_ge(e_done, u + 1)
                if a.second or hd >= 2:
                    act.wait_ge(z_made, u - 1)
                act.activation(w[hd % 2][:], e_ps[hd % 2][:].rearrange("p (t j) -> p t j", t=T), ACT.Relu,
                               scale=-(1.0 - SLOPE)).then_inc(w_made, 1)

            def exp_unit(k, c, hd):
                a, hd = unit(k, c, hd, 0)
                if not a.real:
                    return
                u = a.q * H + hd
                act.wait_ge(nmax_made, u + 1)
                if a.second or hd >= 2:
                    act.wait_ge(pT_done, u - 1)
                if hd == 0 and a.third:
                    act.wait_ge(outn_made, a.q - 1)
                for t in range(T):
                    last = act.activation(p[hd % 2][:, t, :], z[hd % 2][:, t, :], ACT.Exp, bias=nmax[hd % 2][:, t:t + 1],
                                          accum_out=den[a.par][:, hd, t:t + 1])
                last.then_inc(p_made, 1)

            def step(k, c):
                f, b, r = At(k, c), At(k, c - 2), At(k, c - 3)
                for s in range(H):
                    relu_unit(k, c, s)
                    if s == 0:
                        if r.real:
                            act.wait_ge(xn2T_done, r.q + 1)
                            if r.second:
                                act.wait_ge(gate_done, r.q)
                            copy(xn2T[:], seven[:].rearrange("p (t n) -> p t n", t=T)).then_inc(xn2T_made, 1)
                    if s == 1:
                        if f.real:
                            act.wait_ge(xnT_done, f.q + 1)
                            if f.second:
                                act.wait_ge(h_done, f.q)
                            copy(xnT[:], five[:].rearrange("p (t n) -> p t n", t=T)).then_inc(xnT_made, 1)
                    if s == 2:
                        if f.real:
                            act.wait_ge(h_done, f.q + 1)
                            if f.third:
                                act.wait_ge(pv_done, H * (f.q - 1))
                            for i, ps in enumerate((five, six)):
                                last = copy(h[f.par][:, 2 * i:2 * i + 2, :],
                                            ps[:, 0:2 * HW].rearrange("p (t n) -> p t n", t=2)[:, :, 0:P])
                            last.then_inc(h_made, 1)
                        if r.real:
                            act.wait_ge(lsh_made, r.q + 1)
                            if r.second:
                                act.wait_ge(member_made, r.q)
                            act.activation(ex[:], lsh[:], ACT.Exp).then_inc(ex_made, 1)
                    if s == 3 and f.real:
                        act.wait_ge(adj_in[f.par], 16 * (f.half + 1))
                        if f.third:
                            act.wait_ge(e_done, H * (f.q - 1))
                        act.activation(mask[f.par][:], xg(adj_all, f), ACT.Copy, scale=BIG, bias=-BIG).then_inc(mask_made, 1)
                    exp_unit(k, c, s)

            steps(act, step)

            def gelu(k, j, x_, first):
                u = (k * UNROLL + j) * 2 + x_
                act.wait_ge(up_done, u + 1)
                if not first:
                    act.wait_ge(down_done, u - 1)
                act.wait_ge(staged, u + 1)
                for i in range(FC):
                    last = act.activation(gT[x_][:, i, :], e_ps[x_][:, i * P:(i + 1) * P], ACT.Gelu,
                                          bias=WS[j % 2][x_][:, B1C + i:B1C + i + 1])
                last.then_inc(gelu_made, 1)

            def turn(k, first):
                for j in range(UNROLL):
                    for x_ in range(2):
                        gelu(k, j, x_, first and j == 0)

            turn(0, True)
            with act.Fori(1, TILES // UNROLL) as k:
                turn(k, False)

        @block.tensor
        def _(pe):
            mm, tr = nc.tensor.matmul, nc.tensor.transpose

            pe.wait_ge(weights_in, 16 * (2 + 2 * H))
            mm(seven[:, 0:2 * H], w_raw[:], att[:], start=True, stop=True).then_inc(wu_ps, 1)
            pe.wait_ge(const_made, 3)
            pe.wait_ge(pool_const, 13)
            pe.wait_ge(wu_made, 1)
            pe.wait_ge(expert_in, 16 * 6)

            def score_unit(k, c, hd):
                a, hd = unit(k, c, hd, 0)
                if not a.real:
                    return
                u = a.q * H + hd
                if hd == 0:
                    pe.wait_ge(mask_made, a.q + 1)
                    pe.wait_ge(rows_made, a.q + 1)
                if a.second or hd >= 2:
                    pe.wait_ge(z_made, u - 1)
                mm(e_ps[hd % 2][:], identb[:], mask[a.par][:].rearrange("p t j -> p (t j)"), start=True, stop=False)
                part = slice(hd * HD, hd * HD + 6)
                for t in range(T):
                    last = mm(e_ps[hd % 2][:, t * P:(t + 1) * P], rows[a.par][part, 0, t, :], rows[a.par][part, 1, t, :],
                              start=False, stop=(t == T - 1))
                last.then_inc(e_done, 1)

            def turn_unit(k, c, hd):
                a, hd = unit(k, c, hd, 1)
                if not a.real:
                    return
                u = a.q * H + hd
                pe.wait_ge(p_made, u + 1)
                if a.second or hd >= 2:
                    pe.wait_ge(pT_made, u - 1)
                for t in range(T):
                    last = tr(pT_ps[hd % 2][:, t * P:(t + 1) * P], p[hd % 2][:, t, :], ident[:])
                last.then_inc(pT_done, 1)

            def value_unit(k, c, hd):
                a, hd = unit(k, c, hd, 2)
                if not a.real:
                    return
                u = a.q * H + hd
                pe.wait_ge(pT_made, u + 1)
                if hd == 0:
                    pe.wait_ge(h_made, a.q + 1)
                    if a.second:
                        pe.wait_ge(oT_made, a.q)
                for t in range(T):
                    last = mm(oT_ps[hd * HD:(hd + 1) * HD, t * P:(t + 1) * P], h[a.par][:, t, hd * HD:(hd + 1) * HD],
                              pT[hd % 2][:, t, :], start=True, stop=True)
                last.then_inc(pv_done, 1)

            def step(k, c):
                f, b, r = At(k, c), At(k, c - 2), At(k, c - 3)
                for s in range(H):
                    score_unit(k, c, s)
                    if s == 0 and r.real:
                        pe.wait_ge(xn2_made, r.q + 1)
                        pe.wait_ge(outn_made, r.q + 1)
                        for t in range(T):
                            last = tr(seven[:, t * P:(t + 1) * P], xn2[:, t, :], ident[:])
                        last.then_inc(xn2T_done, 1)
                    if s == 1:
                        if f.real:
                            pe.wait_ge(xn_made, f.q + 1)
                            if f.second:
                                pe.wait_ge(rows_made, f.q)
                            for t in range(T):
                                last = tr(five[:, t * P:(t + 1) * P], xn[f.par][:, t, :], ident[:])
                            last.then_inc(xnT_done, 1)
                        if r.real:
                            pe.wait_ge(xn2T_made, r.q + 1)
                            if r.second:
                                pe.wait_ge(slot_made, r.q)
                            for t in range(T):
                                last = mm(six[:, t * E:(t + 1) * E], xn2T[:, t, :], gw[:], start=True, stop=True)
                            last.then_inc(gate_done, 1)
                    if s == 2:
                        if f.real:
                            pe.wait_ge(xnT_made, f.q + 1)
                            if r.real:
                                pe.wait_ge(lsh_made, r.q + 1)
                            for t in range(T):
                                ps = (five, six)[t // 2]
                                last = mm(ps[:, (t % 2) * HW:(t % 2 + 1) * HW], xnT[:, t, :], wu[:], start=True, stop=True)
                            last.then_inc(h_done, 1)
                        if b.real:
                            pe.wait_ge(oT_made, b.q + 1)
                            if b.second:
                                pe.wait_ge(xn2T_made, b.q)
                            for t in range(T):
                                last = tr(seven[:, t * P:(t + 1) * P], oT[:, t, :], ident[:])
                            last.then_inc(out_done, 1)
                    if s == 3:
                        if f.real:
                            pe.wait_ge(cols_made, f.q + 1)
                            five16 = five[:].bitcast(bf16)
                            for side in range(2):
                                for t in range(T):
                                    at = (side * T + t) * P
                                    last = tr(five16[:, at:at + P],
                                              cols[f.par][:, side * SIDE + t * P:side * SIDE + (t + 1) * P], identb[:])
                            last.then_inc(rows_done, 1)
                        if r.real:
                            pe.wait_ge(member_made, r.q + 1)
                            if f.real:
                                pe.wait_ge(sd_made, f.q + 1)
                            flat = member[:].rearrange("p t g -> p (t g)")
                            mm(six[:, 0:T * PAIRS], before[:], flat, start=True, stop=True)
                            mm(six[:, T * PAIRS:2 * T * PAIRS], ones[:], flat, start=True, stop=True).then_inc(rank_done, 1)
                    turn_unit(k, c, s)
                    value_unit(k, c, s)

            steps(pe, step)

            pe.wait_ge(c_tiles, 14)
            tr(seven[0:4, 0:P], table[:], ident[:]).then_inc(table_done, 1)

            up_ps, down_ps, xT_ps = e_ps, pT_ps, bank[5:7]

            def turn_rows(k, j, first):
                n = k * UNROLL + j
                pe.wait_ge(xn_m, n + 1)
                if not (first and 0 < j < 2 or isinstance(n, int) and n < 2):
                    pe.wait_ge(xT_m, n - 1)
                tr(xT_ps[j % 2][:, 0:P], XN[j % 2][:], ident[:]).then_inc(xT_done, 1)

            def up(k, j, x_, first):
                u = (k * UNROLL + j) * 2 + x_
                if x_ == 0:
                    pe.wait_ge(xT_m, k * UNROLL + j + 1)
                pe.wait_ge(staged, u + 1)
                if not first:
                    pe.wait_ge(gelu_made, u - 1)
                for i in range(FC):
                    last = mm(up_ps[x_][:, i * P:(i + 1) * P], WS[j % 2][x_][:, i * P:(i + 1) * P], XT[j % 2][:], start=True, stop=True)
                last.then_inc(up_done, 1)

            def down(k, j, x_, first):
                u = (k * UNROLL + j) * 2 + x_
                if not first:
                    pe.wait_ge(combined, u - 1)
                mm(down_ps[x_][:, 0:P], ones[0:3, :], WS[j % 2][x_][0:3, B2C:EXP].bitcast(bf16), start=True, stop=False)
                pe.wait_ge(gelu_made, u + 1)
                for i in range(FC):
                    last = mm(down_ps[x_][:, 0:P], gT[x_][:, i, :], WS[j % 2][x_][:, W2C + i * P:W2C + (i + 1) * P],
                              start=False, stop=(i == FC - 1))
                last.then_inc(down_done, 1)

            turn_rows(0, 0, True)
            up(0, 0, 0, True)

            def turn(k, first, last):
                for j in range(UNROLL):
                    start = first and j == 0
                    after = (k, j + 1) if j + 1 < UNROLL else None if last else (k + 1, 0)
                    if after:
                        turn_rows(*after, first)
                    up(k, j, 1, start)
                    down(k, j, 0, start)
                    if after:
                        up(*after, 0, False)
                    down(k, j, 1, start)

            turn(0, True, False)
            with pe.Fori(1, TILES // UNROLL - 1) as k:
                turn(k, False, False)
            turn(TILES // UNROLL - 1, False, True)

        @block.vector
        def _(dve):
            tt, ts, stt = dve.tensor_tensor, dve.tensor_scalar, dve.scalar_tensor_tensor
            ln1, split, norm = Chain(dve, c_ln1, T), Chain(dve, c_split, 4), Chain(dve, c_norm, 1)
            ln2, gate, topc, slots = Chain(dve, c_ln2, T), Chain(dve, c_gate, 2), Chain(dve, c_top, 15), Chain(dve, c_slot, 7)

            dve.memset(att[:], 0.0).then_inc(cols_set, 1)
            for par in range(2):
                dve.memset(cols[par][:], 0.0).then_inc(cols_set, 1)
            dve.wait_ge(cols_set, 3)
            for par in range(2):
                for side in range(2):
                    at = side * SIDE + 3 * (1 - side)
                    v = cols[par][:, side * SIDE:(side + 1) * SIDE].rearrange("p (n w) -> p n w", w=32)
                    dve.memset(v[:, :, 3 * (1 - side):3 * (1 - side) + 3], 1.0).then_inc(cols_set, 1)
            b2c = Chain(dve, b2_chain, 8)
            b2c.start(0)
            dve.wait_ge(b2_in, 16)
            dve.wait_ge(pool_const, 13)
            hi = b2w[:, 3, :].bitcast(bf16)
            v, r1, r2, s1 = b2w[:, 0, :], b2w[:, 1, :], b2w[:, 2, :], b2w[:, 4, :]
            c1, c2 = hi[:, 0:E * P], hi[:, E * P:2 * E * P]
            b2c.link(dve.tensor_copy(c1, v))
            b2c.link(tt(r1, v, c1, ALU.subtract))
            b2c.link(dve.tensor_copy(c2, r1))
            b2c.link(tt(r2, r1, c2, ALU.subtract))
            b2c.link(ts(s1, c1, ident[0:3, 0:1], None, ALU.mult))
            b2c.link(stt(s1, c2, ident[0:3, 1:2], s1, ALU.mult, ALU.add))
            b2c.link(stt(s1, r2, ident[0:3, 2:3], s1, ALU.mult, ALU.add))
            b2c.link(dve.memset(experts[:, :, B2C:EXP], 0.0))
            dve.tensor_copy(experts[0:3, :, B2C:EXP].bitcast(bf16),
                            s1.rearrange("p (e d) -> p e d", e=E)).then_inc(b2_in, 1)
            dve.wait_ge(wu_ps, 1)
            dve.tensor_copy(wu[:, P:HW], seven[:, 0:2 * H]).then_inc(wu_made, 1)
            dve.wait_ge(cols_set, 7)
            dve.wait_ge(expert_in, 16 * 6)
            dve.wait_ge(const_made, 3)

            def stats(chain, a, bn, mv, src):
                chain.start(a.q)
                for t in range(T):
                    chain.link(dve.bn_stats(bn[:, t, :], src(t)))
                settle(dve)
                for t in range(T - 1):
                    dve.bn_aggr(mv[:, t, :], bn[:, t, :])
                chain.end()
                return dve.bn_aggr(mv[:, T - 1, :], bn[:, T - 1, :])

            def norm1(a):
                dve.wait_ge(x_in[a.par], 16 * (a.half + 1))
                if a.second:
                    dve.wait_ge(xn_made, a.q)
                stats(ln1, a, bn1, mv1, lambda t: x_all[:, bass.ds(a.q * T + t, 1), :].rearrange("p a n -> p (a n)")).then_inc(ln1_made, 1)

            def score_unit(k, c, hd):
                a, hd = unit(k, c, hd, 0)
                if not a.real:
                    return
                u, i = a.q * H + hd, hd % 2
                e = e_ps[i][:].rearrange("p (t j) -> p t j", t=T)
                dve.wait_ge(w_made, u + 1)
                if a.second or hd >= 2:
                    dve.wait_ge(p_made, u - 1)
                tt(z[i][:], e, w[i][:], ALU.add).then_inc(z_made, 1)
                dve.wait_ge(z_made, u + 1)
                dve.tensor_reduce(nmax[i][:], z[i][:], X, ALU.max, negate=True).then_inc(nmax_made, 1)

            def turn_unit(k, c, hd):
                a, hd = unit(k, c, hd, 1)
                if not a.real:
                    return
                u = a.q * H + hd
                dve.wait_ge(pT_done, u + 1)
                if a.second or hd >= 2:
                    dve.wait_ge(pv_done, u - 1)
                dve.tensor_copy(pT[hd % 2][:], pT_ps[hd % 2][:].rearrange("p (t j) -> p t j", t=T)).then_inc(pT_made, 1)

            def take_sd(a):
                split.start(a.q)
                dve.wait_ge(h_made, a.q + 1)
                sdv = sd[:].rearrange("p s (t h) -> p s t h", t=T)
                for i, ps in enumerate((five, six)):
                    src = ps[:, 0:2 * HW].rearrange("p (t n) -> p t n", t=2)[:, :, P:HW]
                    ins = dve.tensor_copy(sdv[:, :, 2 * i:2 * i + 2, :], src.rearrange("p t (s h) -> p s t h", s=2))
                    if i == 1:
                        ins.then_inc(sd_made, 1)
                dve.wait_ge(sd_made, a.q + 1)
                if a.third:
                    dve.wait_ge(rows_done, a.q - 1)
                place = cols[a.par][:].rearrange("p (s r) -> p s r", s=2)[:, :, 0:SIDE].rearrange("p s (n w) -> p s n w", w=32)
                part = [place[:, :, :, i] for i in range(3)]
                split.link(dve.tensor_copy(part[0], sd[:]))
                split.link(tt(sd_rest[:, 0], sd[:], part[0], ALU.subtract))
                split.link(dve.tensor_copy(part[1], sd_rest[:, 0]))
                split.link(tt(sd_rest[:, 1], sd_rest[:, 0], part[1], ALU.subtract))
                dve.tensor_copy(part[2], sd_rest[:, 1]).then_inc(cols_made, 1)
                split.end()

            def step(k, c):
                f, b, r = At(k, c), At(k, c - 2), At(k, c - 3)
                for s in range(H):
                    score_unit(k, c, s)
                    turn_unit(k, c, s)
                    if s == 0 and At(k, c + 1).real:
                        norm1(At(k, c + 1))
                    if s == 1:
                        if b.real:
                            dve.wait_ge(pv_done, H * (b.q + 1))
                            if b.second:
                                dve.wait_ge(out_done, b.q)
                            dve.tensor_copy(oT[:], oT_ps[:].rearrange("p (t n) -> p t n", t=T)).then_inc(oT_made, 1)
                        if r.real:
                            gate.start(r.q)
                            dve.wait_ge(gate_done, r.q + 1)
                            gate.link(tt(lg[:], six[:, 0:T * E].rearrange("p (t e) -> p t e", t=T),
                                         gbias[:].unsqueeze(1).broadcast_to([P, T, E]), ALU.add))
                            gate.link(dve.reduce_max(lmax[:], lg[:], X))
                            gate.end()
                            if r.second:
                                dve.wait_ge(ex_made, r.q)
                            tt(lsh[:], lg[:], lmax[:].unsqueeze(2).broadcast_to([P, T, E]), ALU.subtract).then_inc(lsh_made, 1)
                    if s == 2:
                        if f.real:
                            take_sd(f)
                        if b.real:
                            norm.start(b.q)
                            dve.wait_ge(p_made, H * (b.q + 1))
                            norm.link(dve.reciprocal(rden[:], den[b.par][:]))
                            dve.wait_ge(out_done, b.q + 1)
                            if b.second:
                                dve.wait_ge(x2_made, b.q)
                            tt(outn[:].rearrange("p t (h n) -> p t h n", h=H),
                               seven[:].rearrange("p (t h n) -> p t h n", t=T, h=H),
                               rden[:].rearrange("p h t -> p t h").unsqueeze(3).broadcast_to([P, T, H, HD]),
                               ALU.mult).then_inc(outn_made, 1)
                            norm.end()
                        if r.real:
                            route(r)
                    if s == 3:
                        if f.real:
                            dve.wait_ge(rows_done, f.q + 1)
                            if f.third:
                                dve.wait_ge(e_done, H * (f.q - 1))
                            dve.tensor_copy(rows[f.par][:].rearrange("p s t n -> p (s t n)"),
                                            five[:].bitcast(bf16)).then_inc(rows_made, 1)
                        if b.real:
                            dve.wait_ge(x2_made, b.q + 1)
                            if b.second:
                                dve.wait_ge(xn2_made, b.q)
                            R_ = R[b.par]
                            stats(ln2, b, bn2, mv2, lambda t: R_[:, t, 0:P]).then_inc(c_mean, 1)
                            dve.wait_ge(c_mean, b.q + 1)
                            dve.tensor_copy(R_[:, :, MEAN], mv2[:, :, 0]).then_inc(ln2_made, 1)
                        if r.real:
                            place_rows(r)

            def route(r):
                topc.start(r.q)
                over = lambda v: v.unsqueeze(2).broadcast_to([P, T, E])
                dve.wait_ge(ex_made, r.q + 1)
                topc.link(dve.reduce_sum(esum[:, 0, :], ex[:], X))
                topc.link(dve.reciprocal(esum[:, 1, :], esum[:, 0, :]))
                topc.link(tt(prob[:], ex[:], over(esum[:, 1, :]), ALU.mult))

                def first_of(src, dst):
                    topc.link(dve.reduce_max(best[:], src[:], X))
                    topc.link(tt(tie[:, 0], src[:], over(best[:]), ALU.is_equal))
                    topc.link(tt(tie[:, 1], tie[:, 0], descend[:], ALU.mult))
                    topc.link(dve.reduce_max(best[:], tie[:, 1], X))
                    return tt(dst, tie[:, 1], over(best[:]), ALU.is_equal)

                topc.link(first_of(prob, top[:, 0]))
                topc.link(stt(left[:], top[:, 0], -4.0, prob[:], ALU.mult, ALU.add))
                topc.link(first_of(left, top[:, 1]))
                topc.link(tt(top[:, 2], top[:, 0], top[:, 1], ALU.add))
                topc.end()
                if r.second:
                    dve.wait_ge(rank_done, r.q)
                tt(R[r.par][:, :, CW:CW + E], prob[:], top[:, 2], ALU.mult)
                ts(R[r.par][:, :, ID], R[r.par][:, :, ID], float(2 * T * P), None, ALU.add)
                at = 0
                for i in range(E - 1):
                    n = E - 1 - i
                    last = tt(member[:, :, at:at + n], top[:, 2, :, i:i + 1].broadcast_to([P, T, n]),
                              top[:, 2, :, i + 1:E], ALU.mult)
                    at += n
                last.then_inc(member_made, 1)

            def place_rows(r):
                slots.start(r.q)
                dve.wait_ge(rank_done, r.q + 1)
                ahead = six[:, 0:T * PAIRS].rearrange("p (t g) -> p t g", t=T)
                total = six[:, T * PAIRS:2 * T * PAIRS].rearrange("p (t g) -> p t g", t=T)
                for t in range(T):
                    slots.link(tt(run[:, t + 1, :], run[:, t, :], total[:, t, :], ALU.add))
                slots.link(tt(rank[:, 0], run[:, 0:T, :], ahead, ALU.add))
                slots.link(tt(rank[:, 1], rank[:, 0], member[:], ALU.mult))
                dve.tensor_copy(run[:, 0, :], run[:, T, :])
                slots.link(dve.reduce_sum(slot[:], rank[:, 1], X))
                slots.end()
                if r.third:
                    dve.wait_ge(scattered[r.par], 16 * T * r.half)
                dve.tensor_copy(slot_i[r.par][:], slot[:]).then_inc(slot_made, 1)

            steps(dve, step)

            tc = Chain(dve, c_tiles, 14)
            tc.start(0)
            dve.wait_ge(slot_made, GROUPS)
            count, cum, start, n_, lt_end, lt_start, mine, at0, one = (tiles[:, i, :] for i in range(9))
            tc.link(tt(count, run[:, 0, :], base[:], ALU.subtract))
            tc.link(ts(count, count, float(P - 1), None, ALU.add))
            tc.link(dve.tensor_copy(tiles_i[:, 0, :], count))
            tc.link(ts(tiles_i[:, 1, :], tiles_i[:, 0, :], P.bit_length() - 1, None, ALU.arith_shift_right))
            tc.link(dve.tensor_copy(n_, tiles_i[:, 1, :]))
            tc.link(dve.memset(one, 1.0))
            tc.link(dve.tensor_tensor_scan(cum, one, n_, 0.0, ALU.mult, ALU.add))
            tc.link(tt(start, cum, n_, ALU.subtract))
            ts(lt_end, cum, number[:], None, ALU.is_le)
            tc.link(ts(lt_start, start, number[:], None, ALU.is_le))
            ts(at0, start, number[:], -float(P), ALU.subtract, ALU.mult)
            tc.link(tt(mine, lt_start, lt_end, ALU.subtract))
            tc.link(stt(at0, at0, -float(DUMMY), base[:], ALU.add, ALU.add))
            tt(tiles[:, 9, :], at0, mine, ALU.mult)
            tt(tiles[:, 10, :], pair_ab[:, 0, :], mine, ALU.mult)
            tc.link(tt(tiles[:, 11, :], pair_ab[:, 1, :], mine, ALU.mult))
            tc.link(dve.reduce_sum(table[:, 0:3], tiles[:, 9:12, :], X))
            dve.memset(table[:, 3:4], 0.0)
            tc.link(ts(table[:, 0:1], table[:, 0:1], float(DUMMY), None, ALU.add))
            tc.end()
            dve.tensor_copy(ends_i[:], run[0:1, 0, :])
            dve.wait_ge(table_done, 1)
            dve.tensor_copy(table_i[:], seven[0:4, 0:P]).then_inc(table_made, 1)
            dve.wait_ge(table_made, 1)
            dve.wait_ge(b2_in, 17)

            def stage_expert(k, j, x_, expert, first):
                u = (k * UNROLL + j) * 2 + x_
                if not first:
                    dve.wait_ge(down_done, u - 3)
                dve.tensor_copy(WS[j % 2][x_][:], experts[:, bass.ds(expert, 1), :].rearrange("p a n -> p (a n)")).then_inc(staged, 1)

            def prepare(k, j, first):
                n = k * UNROLL + j
                dve.wait_ge(row_in[j], 16 * (k + 1))
                if not (first and j < 2):
                    dve.wait_ge(xT_done, n - 1)
                ts(XN[j % 2][:], XR[j][:, 0:P], XR[j][:, MEAN:MEAN + 1], XR[j][:, RS:RS + 1], ALU.subtract, ALU.mult).then_inc(xn_m, 1)

            def take_xT(k, j, first):
                n = k * UNROLL + j
                dve.wait_ge(xT_done, n + 1)
                if not (first and j < 2):
                    dve.wait_ge(up_done, 2 * (n - 1))
                dve.tensor_copy(XT[j % 2][:], bank[5 + j % 2][:, 0:P]).then_inc(xT_m, 1)

            def combine(k, j, x_, expert, first):
                u = (k * UNROLL + j) * 2 + x_
                dve.wait_ge(down_done, u + 1)
                if x_ == 1 and not first:
                    dve.wait_ge(y_out[j], 16 * k)
                if x_ == 1:
                    dve.wait_ge(combined, u)
                stt((acc[j % 2], Y[j])[x_][:], pT_ps[x_][:, 0:P],
                    XR[j][:, CW:CW + E][:, bass.ds(expert, 1)], (XR[j][:, 0:P], acc[j % 2][:])[x_],
                    ALU.mult, ALU.add).then_inc(combined, 1)

            def load_experts(k):
                return [[dve.value_load(table_i[1 + x_:2 + x_, bass.ds(k * UNROLL + j, 1)], min_val=0, max_val=E - 1)
                         for x_ in range(2)] for j in range(UNROLL + 1)]

            def turn(k, first):
                def left(n):
                    return not isinstance(k, int) or n < TILES

                chosen = load_experts(k)
                for j in range(UNROLL):
                    n = k * UNROLL + j
                    k1, j1 = (k, j + 1) if j + 1 < UNROLL else (k + 1, 0)
                    k2, j2 = (k, j + 2) if j + 2 < UNROLL else (k + 1, j + 2 - UNROLL)
                    if left(n + 1):
                        take_xT(k1, j1, first and j == 0)
                        stage_expert(k1, j1, 0, chosen[j + 1][0], first and j == 0)
                    combine(k, j, 0, chosen[j][0], first)
                    if left(n + 1):
                        stage_expert(k1, j1, 1, chosen[j + 1][1], first and j == 0)
                    combine(k, j, 1, chosen[j][1], first)
                    if left(n + 2):
                        prepare(k2, j2, False)

            prepare(0, 0, True)
            for x_ in range(2):
                stage_expert(0, 0, x_, load_experts(0)[0][x_], True)
            prepare(0, 1, True)
            take_xT(0, 0, True)
            turn(0, True)
            with dve.Fori(1, TILES // UNROLL - 1) as k:
                turn(k, False)
            turn(TILES // UNROLL - 1, False)


_OUTS = [((64 * 128, 128), 'float32')]


def kernel(x, adj, L0_gnn_W, L0_gnn_att_src, L0_gnn_att_dst, L0_ffn_gate_w, L0_ffn_gate_b, L0_ffn_W1, L0_ffn_b1,
           L0_ffn_W2, L0_ffn_b2):
    import numpy as np
    import concourse.bacc as _bacc
    from concourse import mybir as _mybir
    from concourse.bass_utils import run_bass_kernel_spmd as _run

    G, P, E, F, H = 64, 128, 8, 256, 4
    ready = np.ascontiguousarray
    W = np.asarray(L0_gnn_W)
    ins = {
        "x": ready(np.asarray(x).transpose(1, 0, 2)),
        "adj": ready(np.asarray(adj).transpose(1, 0, 2)),
        "w_rows": ready(W),
        "w_cols": ready(W.T),
        "att_src": ready(np.asarray(L0_gnn_att_src).reshape(H, P // H)),
        "att_dst": ready(np.asarray(L0_gnn_att_dst).reshape(H, P // H)),
        "gate_w": ready(L0_ffn_gate_w),
        "gate_b": ready(L0_ffn_gate_b),
        "w1": ready(np.asarray(L0_ffn_W1).transpose(1, 0, 2)),
        "b1": ready(np.asarray(L0_ffn_b1).reshape(E, F // P, P).transpose(2, 0, 1)),
        "w2": ready(np.asarray(L0_ffn_W2).reshape(E, F // P, P, P).transpose(2, 0, 1, 3).reshape(P, E, F)),
        "b2": ready(np.asarray(L0_ffn_b2).reshape(E * P)),
        "pairs": np.array([[a, b] for a in range(E) for b in range(a + 1, E)], np.float32).T.copy(),
    }
    nc = _bacc.Bacc("TRN2", target_bir_lowering=False, num_devices=1)
    args = [nc.dram_tensor(f"in_{n}", a.shape, _mybir.dt.from_np(a.dtype), kind="ExternalInput").ap()
            for n, a in ins.items()]
    for i, (shape, dtype) in enumerate(_OUTS):
        dt = _mybir.dt.from_np(np.dtype(dtype))
        args.append(nc.dram_tensor(f"out_{i}", shape, dt, kind="ExternalOutput").ap())
    bass_gat_moe_kernel(nc, *args)
    r = _run(nc, [{f"in_{n}": a for n, a in ins.items()}], core_ids=[0])
    return r.results[0]["out_0"].reshape(G, P, P)
```

```python
import concourse.bass as bass
from concourse import mybir
from contextlib import ExitStack


def bass_gat_moe_kernel(nc, x, adj, w_rows, w_cols, att_src, att_dst, gate_w, gate_b, w1, b1, w2, b2,
                        pairs, out):
    f32, bf16 = mybir.dt.float32, mybir.dt.bfloat16
    u32, i32, u8 = mybir.dt.uint32, mybir.dt.int32, mybir.dt.uint8
    ALU, ACT, X = mybir.AluOpType, mybir.ActivationFunctionType, mybir.AxisListType.X

    P = 128
    G = 64
    T = 4
    GROUPS = G // T
    H, HD = 4, 32
    E = 8
    F = 256
    FC = F // P
    PAIRS = E * (E - 1) // 2
    N = G * P
    CAP = N + P
    DUMMY = PAIRS * CAP
    UNROLL = 4
    TILES = -(-((N + PAIRS * (P - 1)) // P) // UNROLL) * UNROLL
    EPS = 1e-5
    SLOPE = 0.2
    BIG = float(2.0 ** 100)
    NOWHERE = float(2 ** 20)
    CW, ID, RS, MEAN, ROW = P, P + E, P + E + 1, P + E + 2, P + E + 4
    W2C, B1C, B2C, EXP = F, F + FC * P, F + FC * P + FC, F + FC * P + FC + P // 2
    HW = P + 2 * H
    AHEAD = T * E
    TOTAL = AHEAD + T * PAIRS

    ctx = ExitStack()
    with ctx:
        def sb(name, shape, dt=f32):
            return ctx.enter_context(nc.sbuf_tensor(name, shape, dt))

        def sem(name):
            return ctx.enter_context(nc.semaphore(name))

        def sems(name, n):
            return [sem(f"{name}{i}") for i in range(n)]

        rows_dram = nc.dram_tensor("rows_by_pair", (DUMMY + P, ROW), f32, kind="Internal").ap()

        ident = sb("ident", [P, P])
        identb = sb("identb", [P, P], bf16)
        before = sb("before", [P, P], bf16)
        ones = sb("ones", [P, P], bf16)
        descend = sb("descend", [P, T, E])
        gbias = sb("gbias", [P, E])
        gw = sb("gw", [P, E])
        wu = sb("wu", [P, HW])
        w_raw = sb("w_raw", [P, P])
        att = sb("att", [P, 2 * H])
        experts = sb("experts", [P, E, EXP])
        b2w = sb("b2w", [3, 5, E * P])
        pair_code = sb("pair_code", [P, PAIRS])
        pad = sb("pad", [P, ROW])
        x_all = sb("x_all", [P, G, P])
        adj_all = sb("adj_all", [P, G, P], u8)
        bn1 = sb("bn1", [P, T, 6])
        mv1 = sb("mv1", [P, T, 2])
        rs1 = sb("rs1", [P, T])
        xs = sb("xs", [P, T, P])
        var_eps = sb("var_eps", [P, T])
        minus_half = sb("minus_half", [P, T])
        xn = [sb(f"xn{i}", [P, T, P]) for i in range(2)]
        xnT = sb("xnT", [P, T, P])
        h = [sb(f"h{i}", [P, T, HW]) for i in range(2)]
        sd_rest = sb("sd_rest", [P, 2, 2, T * H])
        SIDE = T * P
        cols = [sb(f"cols{i}", [P, 2 * (SIDE + 3)], bf16) for i in range(2)]
        rows = [sb(f"rows{i}", [P, 2, T, P], bf16) for i in range(2)]
        mask = [sb(f"mask{i}", [P, T, P], bf16) for i in range(2)]
        nmax = [sb(f"nmax{i}", [P, T]) for i in range(2)]
        w = [sb(f"w{i}", [P, T, P]) for i in range(2)]
        z = [sb(f"z{i}", [P, T, P]) for i in range(2)]
        p = [sb(f"p{i}", [P, T, P]) for i in range(2)]
        pT = [sb(f"pT{i}", [P, T, P]) for i in range(2)]
        den = [sb(f"den{i}", [P, H, T]) for i in range(2)]
        rden = sb("rden", [P, H, T])
        oT = sb("oT", [P, T, P])
        outn = sb("outn", [P, T, P])
        R = [sb(f"R{i}", [P, T, ROW]) for i in range(2)]
        bn2 = sb("bn2", [P, T, 6])
        mv2 = [sb(f"mv2{i}", [P, T, 2]) for i in range(2)]
        rs2 = [sb(f"rs2{i}", [P, T]) for i in range(2)]
        xs2 = sb("xs2", [P, T, P])
        xn2 = sb("xn2", [P, T, P])
        xn2T = sb("xn2T", [P, T, P])
        lg = sb("lg", [P, T, E])
        lmax = sb("lmax", [P, T])
        lsh = sb("lsh", [P, T, E])
        ex = sb("ex", [P, T, E])
        esum = sb("esum", [P, 2, T])
        prob = sb("prob", [P, T, E])
        best = sb("best", [P, T])
        tie = sb("tie", [P, 2, T, E])
        top = sb("top", [P, 3, T, E])
        left = sb("left", [P, T, E])
        member = sb("member", [P, T, PAIRS], bf16)
        run = sb("run", [P, T + 1, PAIRS])
        rank = sb("rank", [P, 2, T, PAIRS])
        slot = sb("slot", [P, T])
        slot_i = [sb(f"slot_i{i}", [P, T], u32) for i in range(2)]
        base = sb("base", [P, PAIRS])
        tiles = sb("tiles", [P, 11, PAIRS])
        tiles_i = sb("tiles_i", [P, 2, PAIRS], i32)
        number = sb("number", [P, 1])
        table = sb("table", [P, 2])
        table_i = sb("table_i", [2, P], i32)
        packed = sb("packed", [1, P // UNROLL])
        packed_i = sb("packed_i", [1, P // UNROLL], i32)
        ends_i = sb("ends_i", [1, PAIRS], i32)
        XR = [sb(f"XR{i}", [P, ROW]) for i in range(UNROLL)]
        XN = [sb(f"XN{i}", [P, P]) for i in range(2)]
        XT = [sb(f"XT{i}", [P, P]) for i in range(2)]
        WS = [[sb(f"WS{i}{x_}", [P, EXP]) for x_ in range(2)] for i in range(2)]
        gT = [sb(f"gT{i}", [P, FC, P]) for i in range(2)]
        acc = [sb(f"acc{i}", [P, P]) for i in range(2)]
        Y = [sb(f"Y{i}", [P, P]) for i in range(UNROLL)]
        row_id = [sb(f"row_id{i}", [P, 1], u32) for i in range(UNROLL)]

        bank = [ctx.enter_context(nc.psum_tensor(f"bank{i}", [P, 512], f32)) for i in range(8)]
        e_ps, pT_ps, oT_ps = bank[0:2], bank[2:4], bank[4]
        five, six, seven = bank[5], bank[6], bank[7]

        const_made, weights_in, wu_ps, wu_made = sem("const_made"), sem("weights_in"), sem("wu_ps"), sem("wu_made")
        pool_const, pad_made = sem("pool_const"), sem("pad_made")
        b2_in, expert_in, b2_chain = sem("b2_in"), sem("expert_in"), sem("b2_chain")
        cols_set = sem("cols_set")
        x_in, adj_in = sems("x_in", 2), sems("adj_in", 2)
        ln1_made, xs_made, xn_made, xnT_done, xnT_made = map(sem, ("ln1_made", "xs_made", "xn_made", "xnT_done", "xnT_made"))
        h_done, h_made, cols_made, rows_done = map(sem, ("h_done", "h_made", "cols_made", "rows_done"))
        rows_made, mask_made = sem("rows_made"), sem("mask_made")
        oT_made, out_done, outn_made, x2_made, ln2_made = map(sem, ("oT_made", "out_done", "outn_made", "x2_made", "ln2_made"))
        xs2_made, xn2_made, xn2T_done, xn2T_made, gate_done = map(sem, ("xs2_made", "xn2_made", "xn2T_done", "xn2T_made", "gate_done"))
        lsh_made, ex_made, member_made, rank_done, slot_made = map(sem, ("lsh_made", "ex_made", "member_made", "rank_done", "slot_made"))
        lg_made, rank_read, row_made = map(sem, ("lg_made", "rank_read", "row_made"))
        scattered = sems("scattered", 2)
        e_done, w_made, z_made, nmax_made, p_made, pT_done, pT_made, pv_done = map(
            sem, ("e_done", "w_made", "z_made", "nmax_made", "p_made", "pT_done", "pT_made", "pv_done"))
        c_ln1, c_split, c_norm, c_ln2, c_gate, c_top, c_slot, c_tiles, c_pack = map(
            sem, ("c_ln1", "c_split", "c_norm", "c_ln2", "c_gate", "c_top", "c_slot", "c_tiles", "c_pack"))
        table_done, table_made, pads_out, ends_made = sem("table_done"), sem("table_made"), sem("pads_out"), sem("ends_made")
        row_in = sems("row_in", UNROLL)
        xn_m, xT_done, xT_m, staged = sem("xn_m"), sem("xT_done"), sem("xT_m"), sem("staged")
        up_done, gelu_made, down_done, combined = sem("up_done"), sem("gelu_made"), sem("down_done"), sem("combined")
        ids_made = sem("ids_made")
        y_out = sems("y_out", UNROLL)

        stands_alone = sem("stands_alone")

        block = ctx.enter_context(nc.Block())

        class Chain:

            def __init__(self, eng, s, length):
                self.eng, self.s, self.length = eng, s, length

            def start(self, turn):
                self.turn, self.n = turn, 0

            def mark(self, instruction):
                self.n += 1
                instruction.then_inc(self.s, 1)

            def wait(self):
                self.eng.wait_ge(self.s, self.turn * self.length + self.n)

            def link(self, instruction):
                self.mark(instruction)
                self.wait()

            def end(self):
                assert self.n == self.length, (self.n, self.length)

        class At:

            def __init__(self, k, c):
                self.q, self.par, self.half, self.c = 2 * k + c, c % 2, k + c // 2, c
                self.static = isinstance(k, int)
                self.real = not self.static or 0 <= self.q < GROUPS
                self.second = not self.static or self.q >= 1
                self.third = not self.static or self.q >= 2

        def steps(eng, step):
            for c in range(-1, 6):
                step(0, c)
            with eng.Fori(3, GROUPS // 2 - 1) as k:
                step(k, 0)
                step(k, 1)
            for c in range(GROUPS - 2, GROUPS + 5):
                step(0, c)

        def unit(k, c, hd, back):
            i = hd - back
            return At(k, c - 1 + i // H), i % H

        def settle(eng):
            eng.sem_inc(stands_alone, 1)

        def xg(tensor, a):
            return tensor[:, bass.ds(a.q * T, T), :]

        BATCH = 7

        def pad_ends(eng, half):
            eng.wait_ge(ends_made, 1)
            with eng.Fori(0, PAIRS // 2 // BATCH) as i:
                ends = [eng.value_load(ends_i[0:1, bass.ds(half * PAIRS // 2 + i * BATCH + j, 1)], min_val=0, max_val=DUMMY - P)
                        for j in range(BATCH)]
                for end in ends:
                    eng.dma_start(rows_dram[bass.ds(end, P), :], pad[:]).then_inc(pads_out, 16)

        @block.sync
        def _(sp):
            sp.dma_start(w_raw[:], w_rows).then_inc(weights_in, 16)
            sp.dma_start(wu[:, 0:P], w_cols).then_inc(weights_in, 16)
            sp.wait_ge(cols_set, 1)
            for hd in range(H):
                part = slice(hd * HD, (hd + 1) * HD)
                sp.dma_start(att[part, hd:hd + 1], att_src[hd, :].rearrange("(p a) -> p a", a=1)).then_inc(weights_in, 16)
                sp.dma_start(att[part, H + hd:H + hd + 1], att_dst[hd, :].rearrange("(p a) -> p a", a=1)).then_inc(weights_in, 16)
            for q in range(2):
                sp.dma_start(x_all[:, q * T:(q + 1) * T, :], x[:, q * T:(q + 1) * T, :]).then_inc(x_in[q], 16)
                sp.dma_start(adj_all[:, q * T:(q + 1) * T, :], adj[:, q * T:(q + 1) * T, :]).then_inc(adj_in[q], 16)
            sp.dma_start(gw[:], gate_w).then_inc(expert_in, 16)
            sp.dma_start(gbias[:], gate_b.partition_broadcast(P)).then_inc(expert_in, 16)
            sp.dma_start(pair_code[:], pairs.partition_broadcast(P)).then_inc(expert_in, 16)
            sp.dma_start(b2w[:, 0, :], b2.partition_broadcast(3)).then_inc(b2_in, 16)
            sp.dma_start(experts[:, :, 0:F], w1).then_inc(expert_in, 16)
            sp.dma_start(experts[:, :, W2C:B1C], w2).then_inc(expert_in, 16)
            sp.dma_start(experts[:, :, B1C:B2C], b1).then_inc(expert_in, 16)
            with sp.Fori(1, GROUPS // 2) as k:
                for par in range(2):
                    at = bass.ds((2 * k + par) * T, T)
                    sp.wait_ge(x_in[par], 16 * k)
                    settle(sp)
                    sp.dma_start(x_all[:, at, :], x[:, at, :]).then_inc(x_in[par], 16)
                    sp.wait_ge(adj_in[par], 16 * k)
                    settle(sp)
                    sp.dma_start(adj_all[:, at, :], adj[:, at, :]).then_inc(adj_in[par], 16)

            sp.wait_ge(pad_made, 1)
            sp.dma_start(rows_dram[DUMMY:DUMMY + P, :], pad[:]).then_inc(pads_out, 16)
            pad_ends(sp, 0)
            sp.wait_ge(table_made, 1)
            for par in range(2):
                sp.wait_ge(scattered[par], 16 * T * GROUPS // 2)
            sp.wait_ge(pads_out, 16 * (PAIRS + 1))

            def fetch(n, j, value):
                sp.dma_start(XR[j][:], rows_dram[bass.ds(value, P), :]).then_inc(row_in[j], 16)

            def starts(n0):
                return [sp.value_load(table_i[1:2, bass.ds(n0 + j, 1)], min_val=0, max_val=DUMMY) for j in range(UNROLL)]

            for j, value in enumerate(starts(0)):
                fetch(j, j, value)
            with sp.Fori(1, TILES // UNROLL) as k:
                for j, value in enumerate(starts(k * UNROLL)):
                    sp.wait_ge(combined, 2 * ((k - 1) * UNROLL + j + 1))
                    sp.wait_ge(ids_made, (k - 1) * UNROLL + j + 1)
                    settle(sp)
                    fetch(k * UNROLL + j, j, value)
            for j in range(UNROLL):
                sp.wait_ge(y_out[j], 16 * (TILES // UNROLL))

        @block.gpsimd
        def _(pool):
            pool.memset(ident[:], 0.0).then_inc(pool_const, 1)
            pool.memset(ones[:], 1.0).then_inc(pool_const, 1)
            pool.memset(before[:], 1.0).then_inc(pool_const, 1)
            pool.wait_ge(pool_const, 3)
            pool.affine_select(out=ident[:], in_=ident[:], compare_op=ALU.not_equal, fill=1.0, base=0,
                               pattern=[[-1, P]], channel_multiplier=1).then_inc(pool_const, 1)
            pool.affine_select(out=before[:], in_=before[:], compare_op=ALU.is_gt, fill=0.0, base=0,
                               pattern=[[1, P]], channel_multiplier=-1).then_inc(pool_const, 1)
            pool.iota(descend[:], pattern=[[0, T], [-1, E]], base=E, channel_multiplier=0,
                      allow_small_or_imprecise_dtypes=True).then_inc(pool_const, 1)
            pool.iota(number[:], pattern=[[0, 1]], base=0, channel_multiplier=1,
                      allow_small_or_imprecise_dtypes=True).then_inc(pool_const, 1)
            pool.iota(base[:], pattern=[[CAP, PAIRS]], base=0, channel_multiplier=0,
                      allow_small_or_imprecise_dtypes=True).then_inc(pool_const, 1)
            pool.iota(run[:, 0, :], pattern=[[CAP, PAIRS]], base=0, channel_multiplier=0,
                      allow_small_or_imprecise_dtypes=True).then_inc(pool_const, 1)
            for par in range(2):
                pool.memset(R[par][:], 0.0).then_inc(pool_const, 1)
            pool.memset(pad[:], 0.0).then_inc(pool_const, 1)
            pool.memset(minus_half[:], -0.5).then_inc(pool_const, 1)
            pool.wait_ge(pool_const, 13)
            for par in range(2):
                pool.iota(R[par][:, :, ID], pattern=[[P, T]], base=(par - 2) * T * P, channel_multiplier=1,
                          allow_small_or_imprecise_dtypes=True).then_inc(const_made, 1)
            pool.memset(pad[:, ID:ID + 1], NOWHERE).then_inc(pad_made, 1)
            pool.tensor_copy(identb[:], ident[:]).then_inc(const_made, 1)

            def normalize(dst, mid, src, mv, rstd, mid_made, a):
                over = lambda v: v.unsqueeze(2).broadcast_to([P, T, P])
                settle(pool)
                pool.tensor_scalar(var_eps[:], mv[:, :, 1], EPS, None, ALU.add).then_inc(mid_made, 1)
                pool.tensor_tensor(mid[:], src, over(mv[:, :, 0]), ALU.subtract).then_inc(mid_made, 1)
                pool.wait_ge(mid_made, 3 * a.q + 2)
                pool.tensor_tensor(rstd, var_eps[:], minus_half[:], ALU.pow).then_inc(mid_made, 1)
                pool.wait_ge(mid_made, 3 * (a.q + 1))
                return pool.tensor_tensor(dst[:], mid[:], over(rstd), ALU.mult)

            def step(k, c):
                n, b, v, m = At(k, c + 1), At(k, c - 2), At(k, c - 3), At(k, c - 5)
                if v.real:
                    pool.wait_ge(ln2_made, v.q + 1)
                    if v.second:
                        pool.wait_ge(xn2T_done, v.q)
                    if v.third:
                        pool.wait_ge(row_made, v.q - 1)
                    normalize(xn2, xs2, xg(x_all, v), mv2[v.par], rs2[v.par][:], xs2_made, v).then_inc(xn2_made, 1)
                if m.real:
                    pool.wait_ge(slot_made, m.q + 1)
                    settle(pool)
                    for t in range(T):
                        pool.indirect_dma_start(
                            rows_dram, bass.IndirectOffsetOnAxis(ap=slot_i[m.par][:, t:t + 1], axis=0),
                            R[m.par][:, t, :], None).then_inc(scattered[m.par], 16)
                if n.real:
                    pool.wait_ge(ln1_made, n.q + 1)
                    if n.third:
                        pool.wait_ge(xnT_done, n.q - 1)
                    normalize(xn[n.par], xs, xg(x_all, n), mv1, rs1[:], xs_made, n).then_inc(xn_made, 1)
                if b.real:
                    pool.wait_ge(outn_made, b.q + 1)
                    pool.tensor_tensor(xg(x_all, b), outn[:], xg(x_all, b), ALU.add).then_inc(x2_made, 1)

            steps(pool, step)

            def place(k, j, first):
                n = k * UNROLL + j
                pool.wait_ge(row_in[j], 16 * (k + 1))
                if not first:
                    pool.wait_ge(y_out[j], 16 * k)
                settle(pool)
                pool.tensor_copy(row_id[j][:], XR[j][:, ID:ID + 1]).then_inc(ids_made, 1)
                pool.wait_ge(ids_made, n + 1)
                pool.wait_ge(combined, 2 * (n + 1))
                settle(pool)
                pool.indirect_dma_start(out, bass.IndirectOffsetOnAxis(ap=row_id[j][:], axis=0), Y[j][:], None,
                                        bounds_check=N - 1, oob_is_err=False).then_inc(y_out[j], 16)

            for j in range(UNROLL):
                place(0, j, True)
            with pool.Fori(1, TILES // UNROLL) as k:
                for j in range(UNROLL):
                    place(k, j, False)

        @block.scalar
        def _(act):
            def copy(dst, src):
                return act.activation(dst, src, ACT.Copy)

            def relu_unit(k, c, hd):
                a, hd = unit(k, c, hd, 0)
                if not a.real:
                    return
                u = a.q * H + hd
                act.wait_ge(e_done, u + 1)
                if a.second or hd >= 2:
                    act.wait_ge(z_made, u - 1)
                act.activation(w[hd % 2][:], e_ps[hd % 2][:].rearrange("p (t j) -> p t j", t=T), ACT.Relu,
                               scale=-(1.0 - SLOPE)).then_inc(w_made, 1)

            def exp_unit(k, c, hd):
                a, hd = unit(k, c, hd, 1)
                if not a.real:
                    return
                u = a.q * H + hd
                act.wait_ge(nmax_made, u + 1)
                if a.second or hd >= 2:
                    act.wait_ge(pT_done, u - 1)
                if hd == 0 and a.third:
                    act.wait_ge(outn_made, a.q - 1)
                for t in range(T):
                    last = act.activation(p[hd % 2][:, t, :], z[hd % 2][:, t, :], ACT.Exp, bias=nmax[hd % 2][:, t:t + 1],
                                          accum_out=den[a.par][:, hd, t:t + 1])
                last.then_inc(p_made, 1)

            def pT_unit(k, c, hd):
                a, hd = unit(k, c, hd, 1)
                if not a.real:
                    return
                u = a.q * H + hd
                act.wait_ge(pT_done, u + 1)
                if a.second or hd >= 2:
                    act.wait_ge(pv_done, u - 1)
                copy(pT[hd % 2][:], pT_ps[hd % 2][:].rearrange("p (t j) -> p t j", t=T)).then_inc(pT_made, 1)

            def step(k, c):
                f, b, v, r = At(k, c), At(k, c - 2), At(k, c - 3), At(k, c - 4)
                for s in range(H):
                    exp_unit(k, c, s)
                    relu_unit(k, c, s)
                    if s == 0 and r.real:
                        act.wait_ge(xn2T_done, r.q + 1)
                        if r.second:
                            act.wait_ge(gate_done, r.q)
                        copy(xn2T[:], seven[:].rearrange("p (t n) -> p t n", t=T)).then_inc(xn2T_made, 1)
                    if s == 1:
                        if f.real:
                            act.wait_ge(xnT_done, f.q + 1)
                            if f.second:
                                act.wait_ge(h_done, f.q)
                            copy(xnT[:], five[:].rearrange("p (t n) -> p t n", t=T)).then_inc(xnT_made, 1)
                        if b.real:
                            act.wait_ge(pv_done, H * (b.q + 1))
                            if b.second:
                                act.wait_ge(out_done, b.q)
                            copy(oT[:], oT_ps[:].rearrange("p (t n) -> p t n", t=T)).then_inc(oT_made, 1)
                        if r.real:
                            act.wait_ge(lsh_made, r.q + 1)
                            if r.second:
                                act.wait_ge(member_made, r.q)
                            act.activation(ex[:], lsh[:], ACT.Exp).then_inc(ex_made, 1)
                    if s == 2 and f.real:
                        act.wait_ge(h_done, f.q + 1)
                        if f.third:
                            act.wait_ge(pv_done, H * (f.q - 1))
                            act.wait_ge(cols_made, f.q - 1)
                        for i, ps in enumerate((five, six)):
                            last = copy(h[f.par][:, 2 * i:2 * i + 2, :],
                                        ps[:, 0:2 * HW].rearrange("p (t n) -> p t n", t=2))
                        last.then_inc(h_made, 1)
                    if s == 3 and f.real:
                        act.wait_ge(adj_in[f.par], 16 * (f.half + 1))
                        if f.third:
                            act.wait_ge(e_done, H * (f.q - 1))
                        act.activation(mask[f.par][:], xg(adj_all, f), ACT.Copy, scale=BIG, bias=-BIG).then_inc(mask_made, 1)
                    pT_unit(k, c, s)

            steps(act, step)
            pad_ends(act, 1)

            def gelu(k, j, x_, first):
                u = (k * UNROLL + j) * 2 + x_
                act.wait_ge(up_done, u + 1)
                if not first:
                    act.wait_ge(down_done, u - 1)
                act.wait_ge(staged, u + 1)
                for i in range(FC):
                    last = act.activation(gT[x_][:, i, :], e_ps[x_][:, i * P:(i + 1) * P], ACT.Gelu,
                                          bias=WS[j % 2][x_][:, B1C + i:B1C + i + 1])
                last.then_inc(gelu_made, 1)

            def turn(k, first):
                for j in range(UNROLL):
                    for x_ in range(2):
                        gelu(k, j, x_, first and j == 0)

            turn(0, True)
            with act.Fori(1, TILES // UNROLL) as k:
                turn(k, False)

        @block.tensor
        def _(pe):
            mm, tr = nc.tensor.matmul, nc.tensor.transpose

            pe.wait_ge(weights_in, 16 * (2 + 2 * H))
            mm(seven[:, 0:2 * H], w_raw[:], att[:], start=True, stop=True).then_inc(wu_ps, 1)
            pe.wait_ge(const_made, 3)
            pe.wait_ge(pool_const, 13)
            pe.wait_ge(wu_made, 1)
            pe.wait_ge(expert_in, 16 * 6)

            def score_unit(k, c, hd):
                a, hd = unit(k, c, hd, 0)
                if not a.real:
                    return
                u = a.q * H + hd
                if hd == 0:
                    pe.wait_ge(mask_made, a.q + 1)
                    pe.wait_ge(rows_made, a.q + 1)
                if a.second or hd >= 2:
                    pe.wait_ge(z_made, u - 1)
                mm(e_ps[hd % 2][:], identb[:], mask[a.par][:].rearrange("p t j -> p (t j)"), start=True, stop=False)
                part = slice(hd * HD, hd * HD + 6)
                for t in range(T):
                    last = mm(e_ps[hd % 2][:, t * P:(t + 1) * P], rows[a.par][part, 0, t, :], rows[a.par][part, 1, t, :],
                              start=False, stop=(t == T - 1))
                last.then_inc(e_done, 1)

            def turn_unit(k, c, hd):
                a, hd = unit(k, c, hd, 1)
                if not a.real:
                    return
                u = a.q * H + hd
                pe.wait_ge(p_made, u + 1)
                if a.second or hd >= 2:
                    pe.wait_ge(pT_made, u - 1)
                for t in range(T):
                    last = tr(pT_ps[hd % 2][:, t * P:(t + 1) * P], p[hd % 2][:, t, :], ident[:])
                last.then_inc(pT_done, 1)

            def value_unit(k, c, hd):
                a, hd = unit(k, c, hd, 2)
                if not a.real:
                    return
                u = a.q * H + hd
                pe.wait_ge(pT_made, u + 1)
                if hd == 0:
                    pe.wait_ge(h_made, a.q + 1)
                    if a.second:
                        pe.wait_ge(oT_made, a.q)
                for t in range(T):
                    last = mm(oT_ps[hd * HD:(hd + 1) * HD, t * P:(t + 1) * P], h[a.par][:, t, hd * HD:(hd + 1) * HD],
                              pT[hd % 2][:, t, :], start=True, stop=True)
                last.then_inc(pv_done, 1)

            def step(k, c):
                f, b, v, r, m = At(k, c), At(k, c - 2), At(k, c - 3), At(k, c - 4), At(k, c - 5)
                for s in range(H):
                    score_unit(k, c, s)
                    value_unit(k, c, s)
                    if s == 3 and f.real:
                        pe.wait_ge(cols_made, f.q + 1)
                        five16 = five[:].bitcast(bf16)
                        for side in range(2):
                            for t in range(T):
                                at = (side * T + t) * P
                                last = tr(five16[:, at:at + P],
                                          cols[f.par][:, side * SIDE + t * P:side * SIDE + (t + 1) * P], identb[:])
                        last.then_inc(rows_done, 1)
                    turn_unit(k, c, s)
                    if s == 0:
                        if f.real:
                            pe.wait_ge(xn_made, f.q + 1)
                            if f.second:
                                pe.wait_ge(rows_made, f.q)
                            for t in range(T):
                                last = tr(five[:, t * P:(t + 1) * P], xn[f.par][:, t, :], ident[:])
                            last.then_inc(xnT_done, 1)
                        if r.real:
                            pe.wait_ge(xn2T_made, r.q + 1)
                        if m.real:
                            pe.wait_ge(member_made, m.q + 1)
                            flat = member[:].rearrange("p t g -> p (t g)")
                            mm(seven[:, AHEAD:TOTAL], before[:], flat, start=True, stop=True)
                            mm(seven[:, TOTAL:TOTAL + T * PAIRS], ones[:], flat, start=True, stop=True).then_inc(rank_done, 1)
                        if r.real:
                            for t in range(T):
                                last = mm(seven[:, t * E:(t + 1) * E], xn2T[:, t, :], gw[:], start=True, stop=True)
                            last.then_inc(gate_done, 1)
                    if s == 1 and f.real:
                        pe.wait_ge(xnT_made, f.q + 1)
                        for t in range(T):
                            ps = (five, six)[t // 2]
                            last = mm(ps[:, (t % 2) * HW:(t % 2 + 1) * HW], xnT[:, t, :], wu[:], start=True, stop=True)
                        last.then_inc(h_done, 1)
                    if s == 2 and b.real:
                        pe.wait_ge(oT_made, b.q + 1)
                        if r.real:
                            pe.wait_ge(lg_made, r.q + 1)
                        if m.real:
                            pe.wait_ge(rank_read, m.q + 1)
                        for t in range(T):
                            last = tr(seven[:, t * P:(t + 1) * P], oT[:, t, :], ident[:])
                        last.then_inc(out_done, 1)
                    if s == 3 and v.real:
                        pe.wait_ge(xn2_made, v.q + 1)
                        if b.real:
                            pe.wait_ge(outn_made, b.q + 1)
                        else:
                            pe.wait_ge(lg_made, r.q + 1)
                            pe.wait_ge(rank_read, m.q + 1)
                        for t in range(T):
                            last = tr(seven[:, t * P:(t + 1) * P], xn2[:, t, :], ident[:])
                        last.then_inc(xn2T_done, 1)

            steps(pe, step)

            pe.wait_ge(c_tiles, 14)
            tr(seven[0:2, 0:P], table[:], ident[:]).then_inc(table_done, 1)

            up_ps, down_ps, xT_ps = e_ps, pT_ps, bank[5:7]

            def turn_rows(k, j, first):
                n = k * UNROLL + j
                pe.wait_ge(xn_m, n + 1)
                if not (first and 0 < j < 2 or isinstance(n, int) and n < 2):
                    pe.wait_ge(xT_m, n - 1)
                tr(xT_ps[j % 2][:, 0:P], XN[j % 2][:], ident[:]).then_inc(xT_done, 1)

            def up(k, j, x_, first):
                u = (k * UNROLL + j) * 2 + x_
                if x_ == 0:
                    pe.wait_ge(xT_m, k * UNROLL + j + 1)
                pe.wait_ge(staged, u + 1)
                if not first:
                    pe.wait_ge(gelu_made, u - 1)
                for i in range(FC):
                    last = mm(up_ps[x_][:, i * P:(i + 1) * P], WS[j % 2][x_][:, i * P:(i + 1) * P], XT[j % 2][:], start=True, stop=True)
                last.then_inc(up_done, 1)

            def down(k, j, x_, first):
                u = (k * UNROLL + j) * 2 + x_
                if not first:
                    pe.wait_ge(combined, u - 1)
                mm(down_ps[x_][:, 0:P], ones[0:3, :], WS[j % 2][x_][0:3, B2C:EXP].bitcast(bf16), start=True, stop=False)
                pe.wait_ge(gelu_made, u + 1)
                for i in range(FC):
                    last = mm(down_ps[x_][:, 0:P], gT[x_][:, i, :], WS[j % 2][x_][:, W2C + i * P:W2C + (i + 1) * P],
                              start=False, stop=(i == FC - 1))
                last.then_inc(down_done, 1)

            turn_rows(0, 0, True)
            up(0, 0, 0, True)

            def turn(k, first, last):
                for j in range(UNROLL):
                    start = first and j == 0
                    after = (k, j + 1) if j + 1 < UNROLL else None if last else (k + 1, 0)
                    if after:
                        turn_rows(*after, first)
                    up(k, j, 1, start)
                    down(k, j, 0, start)
                    if after:
                        up(*after, 0, False)
                    down(k, j, 1, start)

            turn(0, True, False)
            with pe.Fori(1, TILES // UNROLL - 1) as k:
                turn(k, False, False)
            turn(TILES // UNROLL - 1, False, True)

        @block.vector
        def _(dve):
            tt, ts, stt = dve.tensor_tensor, dve.tensor_scalar, dve.scalar_tensor_tensor
            split, gate, topc, slots = Chain(dve, c_split, 4), Chain(dve, c_gate, 1), Chain(dve, c_top, 15), Chain(dve, c_slot, 7)

            dve.memset(att[:], 0.0).then_inc(cols_set, 1)
            for par in range(2):
                dve.memset(cols[par][:], 0.0).then_inc(cols_set, 1)
            dve.wait_ge(cols_set, 3)
            for par in range(2):
                for side in range(2):
                    at = side * SIDE + 3 * (1 - side)
                    v = cols[par][:, side * SIDE:(side + 1) * SIDE].rearrange("p (n w) -> p n w", w=32)
                    dve.memset(v[:, :, 3 * (1 - side):3 * (1 - side) + 3], 1.0).then_inc(cols_set, 1)
            b2c = Chain(dve, b2_chain, 8)
            b2c.start(0)
            dve.wait_ge(b2_in, 16)
            dve.wait_ge(pool_const, 13)
            hi = b2w[:, 3, :].bitcast(bf16)
            v, r1, r2, s1 = b2w[:, 0, :], b2w[:, 1, :], b2w[:, 2, :], b2w[:, 4, :]
            c1, c2 = hi[:, 0:E * P], hi[:, E * P:2 * E * P]
            b2c.link(dve.tensor_copy(c1, v))
            b2c.link(tt(r1, v, c1, ALU.subtract))
            b2c.link(dve.tensor_copy(c2, r1))
            b2c.link(tt(r2, r1, c2, ALU.subtract))
            b2c.link(ts(s1, c1, ident[0:3, 0:1], None, ALU.mult))
            b2c.link(stt(s1, c2, ident[0:3, 1:2], s1, ALU.mult, ALU.add))
            b2c.link(stt(s1, r2, ident[0:3, 2:3], s1, ALU.mult, ALU.add))
            b2c.link(dve.memset(experts[:, :, B2C:EXP], 0.0))
            dve.tensor_copy(experts[0:3, :, B2C:EXP].bitcast(bf16),
                            s1.rearrange("p (e d) -> p e d", e=E)).then_inc(b2_in, 1)
            dve.wait_ge(wu_ps, 1)
            dve.tensor_copy(wu[:, P:HW], seven[:, 0:2 * H]).then_inc(wu_made, 1)
            dve.wait_ge(cols_set, 7)
            dve.wait_ge(expert_in, 16 * 6)
            dve.wait_ge(const_made, 3)


            def bn(dst, src, done):
                for t in range(T):
                    last = dve.bn_stats(dst[:, t, :], src(t))
                    if t == T - 1:
                        last.then_inc(done, 1)
                    yield

            def aggregate(mv, bn_, done, count):
                dve.wait_ge(done, count)
                settle(dve)
                for t in range(T):
                    last = dve.bn_aggr(mv[:, t, :], bn_[:, t, :])
                return last

            def graph_x(a):
                return lambda t: x_all[:, bass.ds(a.q * T + t, 1), :].rearrange("p a n -> p (a n)")

            def score_unit(k, c, hd, other):
                a, hd = unit(k, c, hd, 0)
                if not a.real:
                    other()
                    return
                u, i = a.q * H + hd, hd % 2
                dve.wait_ge(w_made, u + 1)
                if a.second or hd >= 2:
                    dve.wait_ge(p_made, u - 1)
                tt(z[i][:], e_ps[i][:].rearrange("p (t j) -> p t j", t=T), w[i][:], ALU.add).then_inc(z_made, 1)
                other()
                dve.wait_ge(z_made, u + 1)
                dve.tensor_reduce(nmax[i][:], z[i][:], X, ALU.max, negate=True).then_inc(nmax_made, 1)

            def split_sd(a):
                split.start(a.q)
                dve.wait_ge(h_made, a.q + 1)
                if a.third:
                    dve.wait_ge(rows_done, a.q - 1)
                place = cols[a.par][:].rearrange("p (s r) -> p s r", s=2)[:, :, 0:SIDE].rearrange(
                    "p s (t h w) -> p s t h w", t=T, h=H)
                part = [[place[:, side, :, :, i] for side in range(2)] for i in range(3)]
                sd = [h[a.par][:, :, P + side * H:P + (side + 1) * H] for side in range(2)]
                rest = [[sd_rest[:, i, side, :].rearrange("p (t h) -> p t h", t=T) for side in range(2)] for i in range(2)]
                dve.tensor_copy(part[0][0], sd[0])
                split.mark(dve.tensor_copy(part[0][1], sd[1]))
                yield
                split.wait()
                tt(rest[0][0], sd[0], part[0][0], ALU.subtract)
                split.mark(tt(rest[0][1], sd[1], part[0][1], ALU.subtract))
                yield
                split.wait()
                dve.tensor_copy(part[1][0], rest[0][0])
                split.mark(dve.tensor_copy(part[1][1], rest[0][1]))
                yield
                split.wait()
                tt(rest[1][0], rest[0][0], part[1][0], ALU.subtract)
                split.mark(tt(rest[1][1], rest[0][1], part[1][1], ALU.subtract))
                yield
                split.wait()
                dve.tensor_copy(part[2][0], rest[1][0])
                dve.tensor_copy(part[2][1], rest[1][1]).then_inc(cols_made, 1)
                split.end()

            def step(k, c):
                n, f, b, v, r, m = (At(k, c + i) for i in (1, 0, -2, -3, -4, -5))
                sides = []

                def other():
                    while sides:
                        chain = sides.pop(0)
                        if next(chain, "end") != "end":
                            sides.append(chain)
                            return

                def drain():
                    while sides:
                        other()

                if v.real:
                    dve.wait_ge(x2_made, v.q + 1)
                    if v.third:
                        dve.wait_ge(row_made, v.q - 1)
                    settle(dve)
                    for _ in bn(bn2, graph_x(v), c_ln2):
                        pass
                if r.real:
                    if r.third:
                        dve.wait_ge(scattered[r.par], 16 * T * r.half)
                        settle(dve)
                    dve.tensor_copy(R[r.par][:, :, 0:P], xg(x_all, r))
                if v.real:
                    aggregate(mv2[v.par], bn2, c_ln2, v.q + 1).then_inc(ln2_made, 1)
                score_unit(k, c, 0, other)

                if r.real:
                    sides.append(logits(r))
                if m.real:
                    sides.append(find_slots(m, r))
                for _ in range(6):
                    other()
                if b.real:
                    dve.wait_ge(p_made, H * (b.q + 1))
                    dve.reciprocal(rden[:], den[b.par][:]).then_inc(c_norm, 1)
                other()
                score_unit(k, c, 1, other)
                drain()

                if r.real:
                    sides.append(route(r))
                if n.real:
                    dve.wait_ge(x_in[n.par], 16 * (n.half + 1))
                    if n.second:
                        dve.wait_ge(xn_made, n.q)
                    settle(dve)
                    for _ in bn(bn1, graph_x(n), c_ln1):
                        other()
                    aggregate(mv1, bn1, c_ln1, n.q + 1).then_inc(ln1_made, 1)
                other()
                score_unit(k, c, 2, other)
                if f.real:
                    for _ in split_sd(f):
                        other()

                if b.real:
                    dve.wait_ge(c_norm, b.q + 1)
                    dve.wait_ge(out_done, b.q + 1)
                    if b.second:
                        dve.wait_ge(x2_made, b.q)
                    tt(outn[:].rearrange("p t (h n) -> p t h n", h=H),
                       seven[:].rearrange("p (t h n) -> p t h n", t=T, h=H),
                       rden[:].rearrange("p h t -> p t h").unsqueeze(3).broadcast_to([P, T, H, HD]),
                       ALU.mult).then_inc(outn_made, 1)
                other()
                if f.real:
                    dve.wait_ge(rows_done, f.q + 1)
                    if f.third:
                        dve.wait_ge(e_done, H * (f.q - 1))
                    dve.tensor_copy(rows[f.par][:].rearrange("p s t n -> p (s t n)"), five[:].bitcast(bf16)).then_inc(rows_made, 1)
                other()
                score_unit(k, c, 3, other)
                drain()

            def logits(r):
                gate.start(r.q)
                dve.wait_ge(gate_done, r.q + 1)
                tt(lg[:], seven[:, 0:T * E].rearrange("p (t e) -> p t e", t=T),
                   gbias[:].unsqueeze(1).broadcast_to([P, T, E]), ALU.add).then_inc(lg_made, 1)
                yield
                dve.wait_ge(lg_made, r.q + 1)
                gate.mark(dve.reduce_max(lmax[:], lg[:], X))
                yield
                gate.wait()
                gate.end()
                tt(lsh[:], lg[:], lmax[:].unsqueeze(2).broadcast_to([P, T, E]), ALU.subtract).then_inc(lsh_made, 1)

            def route(r):
                topc.start(r.q)
                over = lambda v: v.unsqueeze(2).broadcast_to([P, T, E])
                dve.wait_ge(ex_made, r.q + 1)
                R_ = R[r.par]
                topc.mark(dve.reduce_sum(esum[:, 0, :], ex[:], X))
                yield
                topc.wait()
                topc.mark(dve.reciprocal(esum[:, 1, :], esum[:, 0, :]))
                yield
                topc.wait()
                topc.mark(tt(prob[:], ex[:], over(esum[:, 1, :]), ALU.mult))
                yield
                topc.wait()
                for src, dst in ((prob, top[:, 0]), (left, top[:, 1])):
                    topc.mark(dve.reduce_max(best[:], src[:], X))
                    yield
                    topc.wait()
                    topc.mark(tt(tie[:, 0], src[:], over(best[:]), ALU.is_equal))
                    yield
                    topc.wait()
                    topc.mark(tt(tie[:, 1], tie[:, 0], descend[:], ALU.mult))
                    yield
                    topc.wait()
                    topc.mark(dve.reduce_max(best[:], tie[:, 1], X))
                    yield
                    topc.wait()
                    topc.mark(tt(dst, tie[:, 1], over(best[:]), ALU.is_equal))
                    yield
                    topc.wait()
                    if src is prob:
                        topc.mark(stt(left[:], top[:, 0], -4.0, prob[:], ALU.mult, ALU.add))
                        yield
                        topc.wait()
                topc.mark(tt(top[:, 2], top[:, 0], top[:, 1], ALU.add))
                ts(R_[:, :, ID], R_[:, :, ID], float(2 * T * P), None, ALU.add)
                yield
                topc.wait()
                topc.end()
                if r.second:
                    dve.wait_ge(rank_read, r.q)
                at = 0
                for i in range(E - 1):
                    n = E - 1 - i
                    last = tt(member[:, :, at:at + n], top[:, 2, :, i:i + 1].broadcast_to([P, T, n]),
                              top[:, 2, :, i + 1:E], ALU.mult)
                    at += n
                last.then_inc(member_made, 1)
                yield
                tt(R_[:, :, CW:CW + E], prob[:], top[:, 2], ALU.mult)
                dve.wait_ge(xn2_made, r.q + 1)
                dve.tensor_copy(R_[:, :, RS], rs2[r.par][:])
                dve.tensor_copy(R_[:, :, MEAN], mv2[r.par][:, :, 0]).then_inc(row_made, 1)

            def find_slots(m, r):
                slots.start(m.q)
                dve.wait_ge(rank_done, m.q + 1)
                if r.real:
                    dve.wait_ge(gate_done, r.q + 1)
                ahead = seven[:, AHEAD:TOTAL].rearrange("p (t g) -> p t g", t=T)
                total = seven[:, TOTAL:TOTAL + T * PAIRS].rearrange("p (t g) -> p t g", t=T)
                for t in range(T):
                    slots.mark(tt(run[:, t + 1, :], run[:, t, :], total[:, t, :], ALU.add))
                    yield
                    slots.wait()
                slots.mark(tt(rank[:, 0], run[:, 0:T, :], ahead, ALU.add))
                yield
                slots.wait()
                dve.tensor_copy(run[:, 0, :], run[:, T, :]).then_inc(rank_read, 1)
                slots.mark(tt(rank[:, 1], rank[:, 0], member[:], ALU.mult))
                yield
                slots.wait()
                slots.mark(dve.reduce_sum(slot[:], rank[:, 1], X))
                yield
                slots.wait()
                slots.end()
                dve.tensor_copy(slot_i[m.par][:], slot[:]).then_inc(slot_made, 1)

            steps(dve, step)

            tc = Chain(dve, c_tiles, 14)
            tc.start(0)
            dve.wait_ge(slot_made, GROUPS)
            count, cum, start, n_, lt_end, lt_start, mine, at0, one = (tiles[:, i, :] for i in range(9))
            dve.tensor_copy(ends_i[:], run[0:1, 0, :]).then_inc(ends_made, 1)
            tc.link(tt(count, run[:, 0, :], base[:], ALU.subtract))
            tc.link(ts(count, count, float(P - 1), None, ALU.add))
            tc.link(dve.tensor_copy(tiles_i[:, 0, :], count))
            tc.link(ts(tiles_i[:, 1, :], tiles_i[:, 0, :], P.bit_length() - 1, None, ALU.arith_shift_right))
            tc.link(dve.tensor_copy(n_, tiles_i[:, 1, :]))
            tc.link(dve.memset(one, 1.0))
            tc.link(dve.tensor_tensor_scan(cum, one, n_, 0.0, ALU.mult, ALU.add))
            tc.link(tt(start, cum, n_, ALU.subtract))
            ts(lt_end, cum, number[:], None, ALU.is_le)
            tc.link(ts(lt_start, start, number[:], None, ALU.is_le))
            ts(at0, start, number[:], -float(P), ALU.subtract, ALU.mult)
            tc.link(tt(mine, lt_start, lt_end, ALU.subtract))
            tc.link(stt(at0, at0, -float(DUMMY), base[:], ALU.add, ALU.add))
            tt(tiles[:, 9, :], pair_code[:], mine, ALU.mult)
            tc.link(tt(tiles[:, 10, :], at0, mine, ALU.mult))
            tc.link(dve.reduce_sum(table[:], tiles[:, 9:11, :], X))
            tc.link(ts(table[:, 1:2], table[:, 1:2], float(DUMMY), None, ALU.add))
            tc.end()
            dve.wait_ge(table_done, 1)
            dve.tensor_copy(table_i[:], seven[0:2, 0:P])
            word = seven[0:1, 0:P].rearrange("r (k j) -> r k j", j=UNROLL)
            pack = Chain(dve, c_pack, UNROLL)
            pack.start(0)
            pack.link(dve.tensor_copy(packed[:], word[:, :, UNROLL - 1]))
            for j in range(UNROLL - 2, -1, -1):
                pack.link(stt(packed[:], packed[:], float(E * E), word[:, :, j], ALU.mult, ALU.add))
            pack.end()
            dve.tensor_copy(packed_i[:], packed[:]).then_inc(table_made, 1)
            dve.wait_ge(table_made, 1)
            dve.wait_ge(b2_in, 17)

            def stage_expert(k, j, x_, expert, first):
                u = (k * UNROLL + j) * 2 + x_
                if not first:
                    dve.wait_ge(down_done, u - 3)
                    settle(dve)
                dve.tensor_copy(WS[j % 2][x_][:], experts[:, bass.ds(expert, 1), :].rearrange("p a n -> p (a n)")).then_inc(staged, 1)

            def prepare(k, j, first):
                n = k * UNROLL + j
                dve.wait_ge(row_in[j], 16 * (k + 1))
                if not (first and j < 2):
                    dve.wait_ge(xT_done, n - 1)
                ts(XN[j % 2][:], XR[j][:, 0:P], XR[j][:, MEAN:MEAN + 1], XR[j][:, RS:RS + 1], ALU.subtract, ALU.mult).then_inc(xn_m, 1)

            def take_xT(k, j, first):
                n = k * UNROLL + j
                dve.wait_ge(xT_done, n + 1)
                if not (first and j < 2):
                    dve.wait_ge(up_done, 2 * (n - 1))
                dve.tensor_copy(XT[j % 2][:], bank[5 + j % 2][:, 0:P]).then_inc(xT_m, 1)

            def combine(k, j, x_, expert, first):
                u = (k * UNROLL + j) * 2 + x_
                dve.wait_ge(down_done, u + 1)
                if x_ == 1 and not first:
                    dve.wait_ge(y_out[j], 16 * k)
                if x_ == 1:
                    dve.wait_ge(combined, u)
                stt((acc[j % 2], Y[j])[x_][:], pT_ps[x_][:, 0:P],
                    XR[j][:, CW:CW + E][:, bass.ds(expert, 1)], (XR[j][:, 0:P], acc[j % 2][:])[x_],
                    ALU.mult, ALU.add).then_inc(combined, 1)

            def load_experts(k):
                found = []
                for word in range(2):
                    experts_of = dve.value_load(packed_i[0:1, bass.ds(k + word, 1)], min_val=0, max_val=2 ** (6 * UNROLL) - 1)
                    for j in range((UNROLL, 1)[word]):
                        found.append([(experts_of >> (6 * j + 3)) & 7, (experts_of >> (6 * j)) & 7])
                return found

            def turn(k, first):
                def left(n):
                    return not isinstance(k, int) or n < TILES

                chosen = load_experts(k)
                for j in range(UNROLL):
                    n = k * UNROLL + j
                    k1, j1 = (k, j + 1) if j + 1 < UNROLL else (k + 1, 0)
                    k2, j2 = (k, j + 2) if j + 2 < UNROLL else (k + 1, j + 2 - UNROLL)
                    if left(n + 1):
                        take_xT(k1, j1, first and j == 0)
                        stage_expert(k1, j1, 0, chosen[j + 1][0], first and j == 0)
                    if left(n + 2):
                        prepare(k2, j2, False)
                    combine(k, j, 0, chosen[j][0], first)
                    if left(n + 1):
                        stage_expert(k1, j1, 1, chosen[j + 1][1], first and j == 0)
                    combine(k, j, 1, chosen[j][1], first)

            prepare(0, 0, True)
            for x_ in range(2):
                stage_expert(0, 0, x_, load_experts(0)[0][x_], True)
            prepare(0, 1, True)
            take_xT(0, 0, True)
            turn(0, True)
            with dve.Fori(1, TILES // UNROLL - 1) as k:
                turn(k, False)
            turn(TILES // UNROLL - 1, False)


_OUTS = [((64 * 128, 128), 'float32')]


def kernel(x, adj, L0_gnn_W, L0_gnn_att_src, L0_gnn_att_dst, L0_ffn_gate_w, L0_ffn_gate_b, L0_ffn_W1, L0_ffn_b1,
           L0_ffn_W2, L0_ffn_b2):
    import numpy as np
    import concourse.bacc as _bacc
    from concourse import mybir as _mybir
    from concourse.bass_utils import run_bass_kernel_spmd as _run

    G, P, E, F, H = 64, 128, 8, 256, 4
    ready = np.ascontiguousarray
    W = np.asarray(L0_gnn_W)
    ins = {
        "x": ready(np.asarray(x).transpose(1, 0, 2)),
        "adj": ready(np.asarray(adj).transpose(1, 0, 2)),
        "w_rows": ready(W),
        "w_cols": ready(W.T),
        "att_src": ready(np.asarray(L0_gnn_att_src).reshape(H, P // H)),
        "att_dst": ready(np.asarray(L0_gnn_att_dst).reshape(H, P // H)),
        "gate_w": ready(L0_ffn_gate_w),
        "gate_b": ready(L0_ffn_gate_b),
        "w1": ready(np.asarray(L0_ffn_W1).transpose(1, 0, 2)),
        "b1": ready(np.asarray(L0_ffn_b1).reshape(E, F // P, P).transpose(2, 0, 1)),
        "w2": ready(np.asarray(L0_ffn_W2).reshape(E, F // P, P, P).transpose(2, 0, 1, 3).reshape(P, E, F)),
        "b2": ready(np.asarray(L0_ffn_b2).reshape(E * P)),
        "pairs": np.array([E * a + b for a in range(E) for b in range(a + 1, E)], np.float32),
    }
    nc = _bacc.Bacc("TRN2", target_bir_lowering=False, num_devices=1)
    args = [nc.dram_tensor(f"in_{n}", a.shape, _mybir.dt.from_np(a.dtype), kind="ExternalInput").ap()
            for n, a in ins.items()]
    for i, (shape, dtype) in enumerate(_OUTS):
        dt = _mybir.dt.from_np(np.dtype(dtype))
        args.append(nc.dram_tensor(f"out_{i}", shape, dt, kind="ExternalOutput").ap())
    bass_gat_moe_kernel(nc, *args)
    r = _run(nc, [{f"in_{n}": a for n, a in ins.items()}], core_ids=[0])
    return r.results[0]["out_0"].reshape(G, P, P)
```

```python
import concourse.bass as bass
from concourse import mybir
from contextlib import ExitStack


def bass_gat_moe_kernel(nc, x, adj, w_rows, w_cols, att_cols, gate_w, gate_b, w1, b1, w2, b2,
                        pairs, out):
    f32, bf16 = mybir.dt.float32, mybir.dt.bfloat16
    u32, i32, u8 = mybir.dt.uint32, mybir.dt.int32, mybir.dt.uint8
    ALU, ACT, X = mybir.AluOpType, mybir.ActivationFunctionType, mybir.AxisListType.X

    P = 128
    G = 64
    T = 4
    GROUPS = G // T
    H, HD = 4, 32
    E = 8
    F = 256
    FC = F // P
    PAIRS = E * (E - 1) // 2
    N = G * P
    CAP = N + P
    DUMMY = PAIRS * CAP
    TILES = (N + PAIRS * (P - 1)) // P
    TURN = 8
    WORD = 4
    PREPARE = 4
    LEAD = 2
    FULL = (TILES - PREPARE) // TURN
    EPS = 1e-5
    SLOPE = 0.2
    BIG = float(2.0 ** 100)
    FAR = 3.0e38
    NOWHERE = float(2 ** 20)
    CW, ID, RS, MEAN, ROW = P, P + E, P + E + 1, P + E + 2, P + E + 4
    W2C, B1C, B2C, EXP = F, F + FC * P, F + FC * P + FC, F + FC * P + FC + P // 2
    HW = P + 2 * H
    AHEAD = T * E
    TOTAL = AHEAD + T * PAIRS

    ctx = ExitStack()
    with ctx:
        def sb(name, shape, dt=f32):
            return ctx.enter_context(nc.sbuf_tensor(name, shape, dt))

        def sem(name):
            return ctx.enter_context(nc.semaphore(name))

        def sems(name, n):
            return [sem(f"{name}{i}") for i in range(n)]

        rows_dram = nc.dram_tensor("rows_by_pair", (DUMMY + P, ROW), f32, kind="Internal").ap()

        ident = sb("ident", [P, P])
        identb = sb("identb", [P, P], bf16)
        before = sb("before", [P, P], bf16)
        ones = sb("ones", [P, P], bf16)
        descend = sb("descend", [P, T, E])
        gbias = sb("gbias", [P, E])
        gw = sb("gw", [P, E])
        wu = sb("wu", [P, HW])
        w_raw = sb("w_raw", [P, P])
        att_raw = sb("att_raw", [P, 2])
        att = sb("att", [P, 2 * H])
        experts = sb("experts", [P, E, EXP])
        B2P = 32
        b2_raw = sb("b2_raw", [B2P, 3, E * P // B2P])
        b2_parts = sb("b2_parts", [B2P, 3, E * P // B2P], bf16)
        pair_code = sb("pair_code", [P, PAIRS])
        pad = sb("pad", [P, ROW])
        x_all = sb("x_all", [P, G, P])
        adj_all = sb("adj_all", [P, G, P], u8)
        bn1 = sb("bn1", [P, T, 6])
        mv1 = sb("mv1", [P, T, 2])
        rs1 = sb("rs1", [P, T])
        xs = sb("xs", [P, T, P])
        var_eps = sb("var_eps", [P, T])
        minus_half = sb("minus_half", [P, T])
        xn = [sb(f"xn{i}", [P, T, P]) for i in range(2)]
        xnT = sb("xnT", [P, T, P])
        h = [sb(f"h{i}", [P, T, HW]) for i in range(2)]
        sd_rest = sb("sd_rest", [P, 2, 2, T * H])
        SIDE = T * P
        cols = [sb(f"cols{i}", [P, 2 * (SIDE + 3)], bf16) for i in range(2)]
        rows = [sb(f"rows{i}", [P, 2, T, P], bf16) for i in range(2)]
        mask = [sb(f"mask{i}", [P, T, P], bf16) for i in range(2)]
        nmax = [sb(f"nmax{i}", [P, T]) for i in range(2)]
        w = [sb(f"w{i}", [P, T, P]) for i in range(2)]
        z = [sb(f"z{i}", [P, T, P]) for i in range(2)]
        p = [sb(f"p{i}", [P, T, P]) for i in range(2)]
        pT = [sb(f"pT{i}", [P, T, P]) for i in range(2)]
        den = [sb(f"den{i}", [P, H, T]) for i in range(2)]
        rden = sb("rden", [P, H, T])
        oT = sb("oT", [P, T, P])
        outn = sb("outn", [P, T, P])
        R = [sb(f"R{i}", [P, T, ROW]) for i in range(2)]
        bn2 = sb("bn2", [P, T, 6])
        mv2 = [sb(f"mv2{i}", [P, T, 2]) for i in range(2)]
        rs2 = [sb(f"rs2{i}", [P, T]) for i in range(2)]
        xs2 = sb("xs2", [P, T, P])
        xn2 = sb("xn2", [P, T, P])
        xn2T = sb("xn2T", [P, T, P])
        lg = sb("lg", [P, T, E])
        lmax = sb("lmax", [P, T])
        lsh = sb("lsh", [P, T, E])
        ex = sb("ex", [P, T, E])
        esum = sb("esum", [P, 2, T])
        prob = sb("prob", [P, T, E])
        best = sb("best", [P, T])
        tie = sb("tie", [P, 2, T, E])
        top = sb("top", [P, 3, T, E])
        left = sb("left", [P, T, E])
        member = sb("member", [P, T, PAIRS], bf16)
        run = sb("run", [P, T + 1, PAIRS])
        rank = sb("rank", [P, 2, T, PAIRS])
        slot = sb("slot", [P, T])
        slot_i = [sb(f"slot_i{i}", [P, T], u32) for i in range(2)]
        base = sb("base", [P, PAIRS])
        tiles = sb("tiles", [P, 15, PAIRS])
        tiles_i = sb("tiles_i", [P, 2, PAIRS], i32)
        number = sb("number", [P, 1])
        table = sb("table", [P, 2])
        again = sb("again", [P, 1])
        hide = sb("hide", [P, P])
        table_i = sb("table_i", [2, P], i32)
        packed = sb("packed", [1, P // WORD])
        packed_i = sb("packed_i", [1, P // WORD], i32)
        XR = [sb(f"XR{i}", [P, ROW]) for i in range(TURN)]
        XN = [sb(f"XN{i}", [P, P]) for i in range(4)]
        XT = [sb(f"XT{i}", [P, P]) for i in range(4)]
        WS = [[sb(f"WS{i}{x_}", [P, EXP]) for x_ in range(2)] for i in range(4)]
        CS = [sb(f"CS{i}", [P, 2]) for i in range(4)]
        gT = [sb(f"gT{i}", [P, FC, P]) for i in range(2)]
        warm = sb("warm", [P, 1])
        acc = [sb(f"acc{i}", [P, P]) for i in range(2)]
        Y = [sb(f"Y{i}", [P, P]) for i in range(TURN)]
        number_of = sb("number_of", [P, 1])
        row_id = [sb(f"row_id{i}", [P, 1], u32) for i in range(TURN)]

        bank = [ctx.enter_context(nc.psum_tensor(f"bank{i}", [P, 512], f32)) for i in range(8)]
        e_ps, pT_ps, oT_ps = bank[0:2], bank[2:4], bank[4]
        five, six, seven = bank[5], bank[6], bank[7]
        up_ps, down_ps, xT_ps = bank[0:2], bank[2:6], bank[6:8]

        const_made, weights_in, wu_ps, wu_made = sem("const_made"), sem("weights_in"), sem("wu_ps"), sem("wu_made")
        pool_const, pad_made = sem("pool_const"), sem("pad_made")
        att_made, starts_made = sem("att_made"), sem("starts_made")
        gate_in, again_made = sem("gate_in"), sem("again_made")
        b2_made, b2_placed = sem("b2_made"), sem("b2_placed")
        b2_in, expert_in, b2_chain = sem("b2_in"), sem("expert_in"), sem("b2_chain")
        cols_set = sem("cols_set")
        x_in, adj_in = sems("x_in", 2), sems("adj_in", 2)
        ln1_made, xs_made, xn_made, xnT_done, xnT_made = map(sem, ("ln1_made", "xs_made", "xn_made", "xnT_done", "xnT_made"))
        h_done, h_made, cols_made, rows_done = map(sem, ("h_done", "h_made", "cols_made", "rows_done"))
        rows_made, mask_made = sem("rows_made"), sem("mask_made")
        oT_made, out_done, outn_made, x2_made, ln2_made = map(sem, ("oT_made", "out_done", "outn_made", "x2_made", "ln2_made"))
        xs2_made, xn2_made, xn2T_done, xn2T_made, gate_done = map(sem, ("xs2_made", "xn2_made", "xn2T_done", "xn2T_made", "gate_done"))
        lsh_made, ex_made, member_made, rank_done, slot_made = map(sem, ("lsh_made", "ex_made", "member_made", "rank_done", "slot_made"))
        lg_made, rank_read, row_made = map(sem, ("lg_made", "rank_read", "row_made"))
        scattered = sems("scattered", 2)
        e_done, w_made, z_made, p_made, pT_done, pT_made, pv_done = map(
            sem, ("e_done", "w_made", "z_made", "p_made", "pT_done", "pT_made", "pv_done"))
        c_ln1, c_split, c_norm, c_ln2, c_gate, c_top, c_slot, c_tiles, c_pack = map(
            sem, ("c_ln1", "c_split", "c_norm", "c_ln2", "c_gate", "c_top", "c_slot", "c_tiles", "c_pack"))
        table_done, table_made, pads_out = sem("table_done"), sem("table_made"), sem("pads_out")
        row_in = sems("row_in", TURN)
        xn_m, xT_done, xT_m, staged = sem("xn_m"), sem("xT_done"), sem("xT_m"), sem("staged")
        up_done, gelu_made, down_done, combined = sem("up_done"), sem("gelu_made"), sem("down_done"), sem("combined")
        ids_made = sem("ids_made")
        y_out = sems("y_out", TURN)
        picked = sem("picked")

        stands_alone = sem("stands_alone")

        block = ctx.enter_context(nc.Block())

        class Chain:

            def __init__(self, eng, s, length):
                self.eng, self.s, self.length = eng, s, length

            def start(self, turn):
                self.turn, self.n = turn, 0

            def mark(self, instruction):
                self.n += 1
                instruction.then_inc(self.s, 1)

            def wait(self):
                self.eng.wait_ge(self.s, self.turn * self.length + self.n)

            def link(self, instruction):
                self.mark(instruction)
                self.wait()

            def end(self):
                assert self.n == self.length, (self.n, self.length)

        class At:

            def __init__(self, k, c):
                self.q, self.par, self.half, self.c = 2 * k + c, c % 2, k + c // 2, c
                self.static = isinstance(k, int)
                self.real = not self.static or 0 <= self.q < GROUPS
                self.second = not self.static or self.q >= 1
                self.third = not self.static or self.q >= 2

        def steps(eng, step):
            for c in range(-1, 6):
                step(0, c)
            with eng.Fori(3, GROUPS // 2 - 1) as k:
                step(k, 0)
                step(k, 1)
            for c in range(GROUPS - 2, GROUPS + 5):
                step(0, c)

        def unit(k, c, hd, back):
            i = hd - back
            return At(k, c - 1 + i // H), i % H

        def settle(eng):
            eng.sem_inc(stands_alone, 1)

        def xg(tensor, a):
            return tensor[:, bass.ds(a.q * T, T), :]

        class Tile:

            def __init__(self, k, j):
                self.n, self.slot, self.turn, self.static = k * TURN + j, j % TURN, k + j // TURN, isinstance(k, int)
                self.real = not self.static or self.n < TILES

            def after(self, back):
                return not self.static or self.n >= back

            def unit(self, x_):
                return 2 * self.n + x_

        def turns(eng, tile):
            for j in range(TURN):
                tile(0, j)
            with eng.Fori(1, FULL) as k:
                for j in range(TURN):
                    tile(k, j)
            for j in range(TILES - FULL * TURN):
                tile(FULL, j)

        @block.sync
        def _(sp):
            for q in range(2):
                sp.dma_start(x_all[:, q * T:(q + 1) * T, :], x[:, q * T:(q + 1) * T, :]).then_inc(x_in[q], 16)
                sp.dma_start(adj_all[:, q * T:(q + 1) * T, :], adj[:, q * T:(q + 1) * T, :]).then_inc(adj_in[q], 16)
            sp.dma_start(gw[:], gate_w).then_inc(gate_in, 16)
            sp.dma_start(gbias[:], gate_b.partition_broadcast(P)).then_inc(gate_in, 16)
            sp.dma_start(pair_code[:], pairs.partition_broadcast(P)).then_inc(expert_in, 16)
            sp.dma_start(b2_raw[:, 0, :], b2.rearrange("(r w) -> r w", r=B2P)).then_inc(b2_in, 16)
            sp.wait_ge(pad_made, 1)
            sp.dma_start(rows_dram[0:DUMMY, :].rearrange("(g c) r -> c g r", c=CAP)[0:P],
                         pad[:].unsqueeze(1).broadcast_to([P, PAIRS, ROW])).then_inc(pads_out, 16)
            sp.dma_start(rows_dram[DUMMY:DUMMY + P, :], pad[:]).then_inc(pads_out, 16)
            sp.dma_start(experts[:, :, 0:F], w1).then_inc(expert_in, 16)
            sp.dma_start(experts[:, :, W2C:B1C], w2).then_inc(expert_in, 16)
            sp.dma_start(experts[:, :, B1C:B2C], b1).then_inc(expert_in, 16)
            sp.wait_ge(b2_made, 1)
            sp.wait_ge(pool_const, 14)
            for i in range(3):
                for e in range(E):
                    per = B2P // E
                    sp.dma_start(experts[i:i + 1, e, B2C:EXP].bitcast(bf16), b2_parts[e * per:(e + 1) * per, i, :]).then_inc(b2_placed, 16)
            with sp.Fori(1, GROUPS // 2) as k:
                for par in range(2):
                    at = bass.ds((2 * k + par) * T, T)
                    sp.wait_ge(x_in[par], 16 * k)
                    settle(sp)
                    sp.dma_start(x_all[:, at, :], x[:, at, :]).then_inc(x_in[par], 16)
                    sp.wait_ge(adj_in[par], 16 * k)
                    settle(sp)
                    sp.dma_start(adj_all[:, at, :], adj[:, at, :]).then_inc(adj_in[par], 16)

            sp.wait_ge(starts_made, 1)

            def fetch(k, j0):
                tiles_ = [Tile(k, j) for j in range(j0, j0 + WORD) if Tile(k, j).real]
                def first_row(a):
                    return sp.value_load(table_i[1:2, bass.ds(a.n + LEAD, 1)], min_val=0, max_val=DUMMY)

                start_up = tiles_[0].static and tiles_[0].n == 0
                values = [first_row(a) for a in tiles_[:1 if start_up else WORD]]
                if start_up:
                    for par in range(2):
                        sp.wait_ge(scattered[par], 16 * T * GROUPS // 2)
                    sp.wait_ge(pads_out, 32)
                for i, a in enumerate(tiles_):
                    value = values[i] if i < len(values) else first_row(a)
                    if a.after(TURN):
                        sp.wait_ge(combined, 2 * (a.n - TURN + 1))
                        sp.wait_ge(ids_made, 2 * (a.n - TURN + 1))
                        settle(sp)
                    sp.dma_start(XR[a.slot][:], rows_dram[bass.ds(value, P), :]).then_inc(row_in[a.slot], 16)

            turns(sp, lambda k, j: fetch(k, j) if j % WORD == 0 else None)
            for j in range(TURN):
                sp.wait_ge(y_out[j], 16 * ((TILES - j + TURN - 1) // TURN))

        @block.gpsimd
        def _(pool):
            pool.memset(ident[:], 0.0).then_inc(pool_const, 1)
            pool.memset(ones[:], 1.0).then_inc(pool_const, 1)
            pool.memset(before[:], 1.0).then_inc(pool_const, 1)
            pool.wait_ge(pool_const, 3)
            pool.affine_select(out=ident[:], in_=ident[:], compare_op=ALU.not_equal, fill=1.0, base=0,
                               pattern=[[-1, P]], channel_multiplier=1).then_inc(pool_const, 1)
            pool.affine_select(out=before[:], in_=before[:], compare_op=ALU.is_gt, fill=0.0, base=0,
                               pattern=[[1, P]], channel_multiplier=-1).then_inc(pool_const, 1)
            pool.iota(descend[:], pattern=[[0, T], [-1, E]], base=E, channel_multiplier=0,
                      allow_small_or_imprecise_dtypes=True).then_inc(pool_const, 1)
            pool.iota(number[:], pattern=[[0, 1]], base=-LEAD, channel_multiplier=1,
                      allow_small_or_imprecise_dtypes=True).then_inc(pool_const, 1)
            pool.iota(base[:], pattern=[[CAP, PAIRS]], base=0, channel_multiplier=0,
                      allow_small_or_imprecise_dtypes=True).then_inc(pool_const, 1)
            pool.iota(run[:, 0, :], pattern=[[CAP, PAIRS]], base=0, channel_multiplier=0,
                      allow_small_or_imprecise_dtypes=True).then_inc(pool_const, 1)
            for par in range(2):
                pool.memset(R[par][:], 0.0).then_inc(pool_const, 1)
            pool.memset(pad[:], 0.0).then_inc(pool_const, 1)
            pool.memset(minus_half[:], -0.5).then_inc(pool_const, 1)
            pool.memset(experts[:, :, B2C:EXP], 0.0).then_inc(pool_const, 1)
            pool.wait_ge(pool_const, 14)
            for par in range(2):
                pool.iota(R[par][:, :, ID], pattern=[[P, T]], base=(par - 2) * T * P, channel_multiplier=1,
                          allow_small_or_imprecise_dtypes=True).then_inc(const_made, 1)
            pool.memset(pad[:, ID:ID + 1], NOWHERE).then_inc(pad_made, 1)
            pool.tensor_copy(identb[:], ident[:]).then_inc(const_made, 1)

            def normalize(dst, mid, src, mv, rstd, mid_made, a):
                over = lambda v: v.unsqueeze(2).broadcast_to([P, T, P])
                settle(pool)
                pool.tensor_scalar(var_eps[:], mv[:, :, 1], EPS, None, ALU.add).then_inc(mid_made, 1)
                pool.tensor_tensor(mid[:], src, over(mv[:, :, 0]), ALU.subtract).then_inc(mid_made, 1)
                pool.wait_ge(mid_made, 3 * a.q + 2)
                pool.tensor_tensor(rstd, var_eps[:], minus_half[:], ALU.pow).then_inc(mid_made, 1)
                pool.wait_ge(mid_made, 3 * (a.q + 1))
                return pool.tensor_tensor(dst[:], mid[:], over(rstd), ALU.mult)

            def residual(b):
                pool.wait_ge(outn_made, b.q + 1)
                pool.tensor_tensor(xg(x_all, b), outn[:], xg(x_all, b), ALU.add).then_inc(x2_made, 1)

            def step(k, c):
                n, b, v, m = At(k, c + 1), At(k, c - 2), At(k, c - 3), At(k, c - 5)
                if v.real:
                    pool.wait_ge(ln2_made, v.q + 1)
                    if v.second:
                        pool.wait_ge(xn2T_done, v.q)
                    if v.third:
                        pool.wait_ge(row_made, v.q - 1)
                    normalize(xn2, xs2, xg(x_all, v), mv2[v.par], rs2[v.par][:], xs2_made, v).then_inc(xn2_made, 1)
                if b.real and not n.real:
                    residual(b)
                if m.real:
                    if not m.second:
                        pool.wait_ge(pads_out, 32)
                    pool.wait_ge(slot_made, m.q + 1)
                    settle(pool)
                    for t in range(T):
                        pool.indirect_dma_start(
                            rows_dram, bass.IndirectOffsetOnAxis(ap=slot_i[m.par][:, t:t + 1], axis=0),
                            R[m.par][:, t, :], None).then_inc(scattered[m.par], 16)
                if n.real:
                    pool.wait_ge(ln1_made, n.q + 1)
                    if n.third:
                        pool.wait_ge(xnT_done, n.q - 1)
                    normalize(xn[n.par], xs, xg(x_all, n), mv1, rs1[:], xs_made, n).then_inc(xn_made, 1)
                if n.real and b.real:
                    residual(b)

            steps(pool, step)

            def place(k, j):
                a = Tile(k, j)
                pool.wait_ge(row_in[a.slot], 16 * (a.turn + 1))
                if a.after(TURN):
                    pool.wait_ge(y_out[a.slot], 16 * a.turn)
                settle(pool)
                pool.tensor_tensor(number_of[:], XR[a.slot][:, ID:ID + 1], hide[:, bass.ds(a.n + LEAD, 1)],
                                   ALU.add).then_inc(ids_made, 1)
                pool.wait_ge(ids_made, 2 * a.n + 1)
                settle(pool)
                pool.tensor_copy(row_id[a.slot][:], number_of[:]).then_inc(ids_made, 1)
                pool.wait_ge(ids_made, 2 * (a.n + 1))
                pool.wait_ge(combined, 2 * (a.n + 1))
                settle(pool)
                pool.indirect_dma_start(out, bass.IndirectOffsetOnAxis(ap=row_id[a.slot][:], axis=0), Y[a.slot][:], None,
                                        bounds_check=N - 1, oob_is_err=False).then_inc(y_out[a.slot], 16)

            pool.wait_ge(table_made, 2)
            turns(pool, place)

        @block.scalar
        def _(act):
            def copy(dst, src):
                return act.activation(dst, src, ACT.Copy)

            act.dma_start(w_raw[:], w_rows).then_inc(weights_in, 16)
            act.dma_start(wu[:, 0:P], w_cols).then_inc(weights_in, 16)
            act.dma_start(att_raw[:], att_cols).then_inc(weights_in, 16)

            def relu_unit(k, c, hd):
                a, hd = unit(k, c, hd, 0)
                if not a.real:
                    return
                u = a.q * H + hd
                act.wait_ge(e_done, u + 1)
                if a.second or hd >= 2:
                    act.wait_ge(z_made, u - 1)
                act.activation(w[hd % 2][:], e_ps[hd % 2][:].rearrange("p (t j) -> p t j", t=T), ACT.Relu,
                               scale=-(1.0 - SLOPE)).then_inc(w_made, 1)

            def exp_unit(k, c, hd):
                a, hd = unit(k, c, hd, 1)
                if not a.real:
                    return
                u = a.q * H + hd
                act.wait_ge(z_made, u + 1)
                if a.second or hd >= 2:
                    act.wait_ge(pT_done, u - 1)
                if hd == 0 and a.third:
                    act.wait_ge(outn_made, a.q - 1)
                for t in range(T):
                    last = act.activation(p[hd % 2][:, t, :], z[hd % 2][:, t, :], ACT.Exp, scale=-1.0, bias=nmax[hd % 2][:, t:t + 1],
                                          accum_out=den[a.par][:, hd, t:t + 1])
                last.then_inc(p_made, 1)

            def pT_unit(k, c, hd):
                a, hd = unit(k, c, hd, 2)
                if not a.real:
                    return
                u = a.q * H + hd
                act.wait_ge(pT_done, u + 1)
                if a.second or hd >= 2:
                    act.wait_ge(pv_done, u - 1)
                copy(pT[hd % 2][:], pT_ps[hd % 2][:].rearrange("p (t j) -> p t j", t=T)).then_inc(pT_made, 1)

            def step(k, c):
                f, b, v, r = At(k, c), At(k, c - 2), At(k, c - 3), At(k, c - 4)
                for s in range(H):
                    if s == 0:
                        relu_unit(k, c, s)
                    exp_unit(k, c, s)
                    pT_unit(k, c, s)
                    if s > 0:
                        relu_unit(k, c, s)
                    if s == 0 and r.real:
                        act.wait_ge(xn2T_done, r.q + 1)
                        if r.second:
                            act.wait_ge(gate_done, r.q)
                        copy(xn2T[:], seven[:].rearrange("p (t n) -> p t n", t=T)).then_inc(xn2T_made, 1)
                    if s == 1:
                        if f.real:
                            act.wait_ge(xnT_done, f.q + 1)
                            if f.second:
                                act.wait_ge(h_done, f.q)
                            copy(xnT[:], five[:].rearrange("p (t n) -> p t n", t=T)).then_inc(xnT_made, 1)
                        if b.real:
                            act.wait_ge(pv_done, H * (b.q + 1))
                            if b.second:
                                act.wait_ge(out_done, b.q)
                            copy(oT[:], oT_ps[:].rearrange("p (t n) -> p t n", t=T)).then_inc(oT_made, 1)
                        if r.real:
                            act.wait_ge(lsh_made, r.q + 1)
                            if r.second:
                                act.wait_ge(member_made, r.q)
                            act.activation(ex[:], lsh[:], ACT.Exp).then_inc(ex_made, 1)
                    if s == 2 and f.real:
                        act.wait_ge(h_done, f.q + 1)
                        if f.third:
                            act.wait_ge(pv_done, H * (f.q - 1))
                            act.wait_ge(cols_made, f.q - 1)
                        for i, ps in enumerate((five, six)):
                            last = copy(h[f.par][:, 2 * i:2 * i + 2, :],
                                        ps[:, 0:2 * HW].rearrange("p (t n) -> p t n", t=2))
                        last.then_inc(h_made, 1)
                    if s == 3 and f.real:
                        act.wait_ge(adj_in[f.par], 16 * (f.half + 1))
                        if f.third:
                            act.wait_ge(e_done, H * (f.q - 1))
                        act.activation(mask[f.par][:], xg(adj_all, f), ACT.Copy, scale=BIG, bias=-BIG).then_inc(mask_made, 1)

            steps(act, step)

            act.activation(warm[:], minus_half[:, 0:1], ACT.Gelu)

            def gelu(k, j, x_):
                a = Tile(k, j)
                u = a.unit(x_)
                act.wait_ge(up_done, u + 1)
                if a.after(1):
                    act.wait_ge(down_done, u - 1)
                act.wait_ge(staged, u + 1)
                for i in range(FC):
                    last = act.activation(gT[x_][:, i, :], up_ps[x_][:, i * P:(i + 1) * P], ACT.Gelu,
                                          bias=WS[j % 4][x_][:, B1C + i:B1C + i + 1])
                last.then_inc(gelu_made, 1)

            def take_xT(k, j):
                a = Tile(k, j)
                if not a.real:
                    return
                act.wait_ge(xT_done, a.n + 1)
                if a.after(4):
                    act.wait_ge(up_done, 2 * (a.n - 3))
                copy(XT[j % 4][:], xT_ps[j % 2][:, 0:P]).then_inc(xT_m, 1)

            def tile(k, j):
                gelu(k, j, 0)
                take_xT(k, j + LEAD)
                gelu(k, j, 1)

            for j in range(LEAD):
                take_xT(0, j)
            turns(act, tile)

        @block.tensor
        def _(pe):
            mm, tr = nc.tensor.matmul, nc.tensor.transpose

            pe.wait_ge(weights_in, 16 * 3)
            pe.wait_ge(att_made, 1)
            mm(seven[:, 0:2 * H], w_raw[:], att[:], start=True, stop=True).then_inc(wu_ps, 1)
            pe.wait_ge(const_made, 3)
            pe.wait_ge(pool_const, 14)

            def score_unit(k, c, hd):
                a, hd = unit(k, c, hd, -1)
                if not a.real:
                    return
                u = a.q * H + hd
                if hd == 0:
                    pe.wait_ge(mask_made, a.q + 1)
                    pe.wait_ge(rows_made, a.q + 1)
                if a.second or hd >= 2:
                    pe.wait_ge(z_made, u - 1)
                mm(e_ps[hd % 2][:], identb[:], mask[a.par][:].rearrange("p t j -> p (t j)"), start=True, stop=False)
                part = slice(hd * HD, hd * HD + 6)
                for t in range(T):
                    last = mm(e_ps[hd % 2][:, t * P:(t + 1) * P], rows[a.par][part, 0, t, :], rows[a.par][part, 1, t, :],
                              start=False, stop=(t == T - 1))
                last.then_inc(e_done, 1)

            def turn_unit(k, c, hd):
                a, hd = unit(k, c, hd, 1)
                if not a.real:
                    return
                u = a.q * H + hd
                pe.wait_ge(p_made, u + 1)
                if a.second or hd >= 2:
                    pe.wait_ge(pT_made, u - 1)
                for t in range(T):
                    last = tr(pT_ps[hd % 2][:, t * P:(t + 1) * P], p[hd % 2][:, t, :], ident[:])
                last.then_inc(pT_done, 1)

            def value_unit(k, c, hd):
                a, hd = unit(k, c, hd, 2)
                if not a.real:
                    return
                u = a.q * H + hd
                pe.wait_ge(pT_made, u + 1)
                if hd == 0:
                    pe.wait_ge(h_made, a.q + 1)
                    if a.second:
                        pe.wait_ge(oT_made, a.q)
                for t in range(T):
                    last = mm(oT_ps[hd * HD:(hd + 1) * HD, t * P:(t + 1) * P], h[a.par][:, t, hd * HD:(hd + 1) * HD],
                              pT[hd % 2][:, t, :], start=True, stop=True)
                last.then_inc(pv_done, 1)

            def step(k, c):
                f, b, v, r, m = At(k, c), At(k, c - 2), At(k, c - 3), At(k, c - 4), At(k, c - 5)
                for s in range(H):
                    if s == 3 and f.real:
                        pe.wait_ge(cols_made, f.q + 1)
                        five16 = five[:].bitcast(bf16)
                        for side in range(2):
                            for t in range(T):
                                at = (side * T + t) * P
                                last = tr(five16[:, at:at + P],
                                          cols[f.par][:, side * SIDE + t * P:side * SIDE + (t + 1) * P], identb[:])
                        last.then_inc(rows_done, 1)
                    if s == 0:
                        if f.real:
                            pe.wait_ge(xn_made, f.q + 1)
                            if f.second:
                                pe.wait_ge(rows_made, f.q)
                            for t in range(T):
                                last = tr(five[:, t * P:(t + 1) * P], xn[f.par][:, t, :], ident[:])
                            last.then_inc(xnT_done, 1)
                        score_unit(k, c, s)
                    turn_unit(k, c, s)
                    value_unit(k, c, s)
                    if 0 < s < H - 1:
                        score_unit(k, c, s)
                    if s == 0:
                        if r.real:
                            pe.wait_ge(xn2T_made, r.q + 1)
                        if m.real:
                            pe.wait_ge(member_made, m.q + 1)
                            flat = member[:].rearrange("p t g -> p (t g)")
                            mm(seven[:, AHEAD:TOTAL], before[:], flat, start=True, stop=True)
                            mm(seven[:, TOTAL:TOTAL + T * PAIRS], ones[:], flat, start=True, stop=True).then_inc(rank_done, 1)
                        if r.real:
                            if not r.second:
                                pe.wait_ge(gate_in, 32)
                            for t in range(T):
                                last = mm(seven[:, t * E:(t + 1) * E], xn2T[:, t, :], gw[:], start=True, stop=True)
                            last.then_inc(gate_done, 1)
                    if s == 1 and f.real:
                        pe.wait_ge(xnT_made, f.q + 1)
                        if not f.second:
                            pe.wait_ge(wu_made, 1)
                        for t in range(T):
                            ps = (five, six)[t // 2]
                            last = mm(ps[:, (t % 2) * HW:(t % 2 + 1) * HW], xnT[:, t, :], wu[:], start=True, stop=True)
                        last.then_inc(h_done, 1)
                    if s == 2 and b.real:
                        pe.wait_ge(oT_made, b.q + 1)
                        if r.real:
                            pe.wait_ge(lg_made, r.q + 1)
                        if m.real:
                            pe.wait_ge(rank_read, m.q + 1)
                        for t in range(T):
                            last = tr(seven[:, t * P:(t + 1) * P], oT[:, t, :], ident[:])
                        last.then_inc(out_done, 1)
                    if s == 3 and v.real:
                        pe.wait_ge(xn2_made, v.q + 1)
                        if b.real:
                            pe.wait_ge(outn_made, b.q + 1)
                        else:
                            pe.wait_ge(lg_made, r.q + 1)
                            pe.wait_ge(rank_read, m.q + 1)
                        for t in range(T):
                            last = tr(seven[:, t * P:(t + 1) * P], xn2[:, t, :], ident[:])
                        last.then_inc(xn2T_done, 1)
                    if s == H - 1:
                        score_unit(k, c, s)

            steps(pe, step)

            pe.wait_ge(c_tiles, 15)
            pe.wait_ge(again_made, 1)
            mm(six[:, 0:P], again[:].broadcast_to([P, P]), ident[:], start=True, stop=True)
            tr(seven[0:2, 0:P], table[:], ident[:]).then_inc(table_done, 1)

            def turn_rows(k, j):
                a = Tile(k, j)
                if not a.real:
                    return
                pe.wait_ge(xn_m, a.n + 1)
                if a.after(2):
                    pe.wait_ge(xT_m, a.n - 1)
                tr(xT_ps[j % 2][:, 0:P], XN[j % 4][:], ident[:]).then_inc(xT_done, 1)

            def up(k, j, x_):
                a = Tile(k, j)
                if not a.real:
                    return
                u = a.unit(x_)
                if x_ == 0:
                    pe.wait_ge(xT_m, a.n + 1)
                pe.wait_ge(staged, u + 1)
                if a.after(1):
                    pe.wait_ge(gelu_made, u - 1)
                for i in range(FC):
                    last = mm(up_ps[x_][:, i * P:(i + 1) * P], WS[j % 4][x_][:, i * P:(i + 1) * P], XT[j % 4][:], start=True, stop=True)
                last.then_inc(up_done, 1)

            def down(k, j, x_):
                a = Tile(k, j)
                u = a.unit(x_)
                ps = [down_ps[(2 * j + i) % 4][:, 0:P] for i in range(2)]
                if x_ == 0:
                    if a.after(2):
                        pe.wait_ge(combined, a.unit(1) - 3)
                    for i in range(2):
                        mm(ps[i], ones[0:3, :], WS[j % 4][i][0:3, B2C:EXP].bitcast(bf16), start=True, stop=False)
                pe.wait_ge(gelu_made, u + 1)
                for i in range(FC):
                    last = mm(ps[x_], gT[x_][:, i, :], WS[j % 4][x_][:, W2C + i * P:W2C + (i + 1) * P],
                              start=False, stop=(i == FC - 1))
                last.then_inc(down_done, 1)

            def tile(k, j):
                turn_rows(k, j + LEAD)
                up(k, j, 1)
                down(k, j, 0)
                up(k, j + 1, 0)
                down(k, j, 1)

            for j in range(LEAD):
                turn_rows(0, j)
            up(0, 0, 0)
            turns(pe, tile)

        @block.vector
        def _(dve):
            tt, ts, stt = dve.tensor_tensor, dve.tensor_scalar, dve.scalar_tensor_tensor
            split, gate, topc, slots = Chain(dve, c_split, 4), Chain(dve, c_gate, 1), Chain(dve, c_top, 15), Chain(dve, c_slot, 7)

            dve.memset(att[:], 0.0).then_inc(cols_set, 1)
            for par in range(2):
                dve.memset(cols[par][:], 0.0).then_inc(cols_set, 1)
            dve.wait_ge(cols_set, 3)
            for par in range(2):
                for side in range(2):
                    at = side * SIDE + 3 * (1 - side)
                    v = cols[par][:, side * SIDE:(side + 1) * SIDE].rearrange("p (n w) -> p n w", w=32)
                    dve.memset(v[:, :, 3 * (1 - side):3 * (1 - side) + 3], 1.0).then_inc(cols_set, 1)
            dve.wait_ge(cols_set, 7)
            dve.wait_ge(weights_in, 16 * 3)
            for hd in range(H):
                part = slice(hd * HD, (hd + 1) * HD)
                last = dve.tensor_copy(att[part, :].rearrange("p (s h) -> p s h", s=2)[:, :, hd], att_raw[part, :])
            last.then_inc(att_made, 1)
            dve.wait_ge(pool_const, 14)
            dve.wait_ge(const_made, 3)


            def bn(dst, src, done):
                for t in range(T):
                    last = dve.bn_stats(dst[:, t, :], src(t))
                    if t == T - 1:
                        last.then_inc(done, 1)
                    yield

            def aggregate(mv, bn_, done, count):
                dve.wait_ge(done, count)
                settle(dve)
                for t in range(T):
                    last = dve.bn_aggr(mv[:, t, :], bn_[:, t, :])
                return last

            def split_b2():
                b2c = Chain(dve, b2_chain, 4)
                b2c.start(0)
                dve.wait_ge(b2_in, 16)
                v, r1, r2 = (b2_raw[:, i, :] for i in range(3))
                c1, c2, c3 = (b2_parts[:, i, :] for i in range(3))
                b2c.link(dve.tensor_copy(c1, v))
                b2c.link(tt(r1, v, c1, ALU.subtract))
                b2c.link(dve.tensor_copy(c2, r1))
                b2c.link(tt(r2, r1, c2, ALU.subtract))
                b2c.end()
                dve.tensor_copy(c3, r2).then_inc(b2_made, 1)

            def graph_x(a):
                return lambda t: x_all[:, bass.ds(a.q * T + t, 1), :].rearrange("p a n -> p (a n)")

            def score_unit(k, c, hd, other):
                a, hd = unit(k, c, hd, 0)
                if not a.real:
                    other()
                    return
                u, i = a.q * H + hd, hd % 2
                dve.wait_ge(w_made, u + 1)
                if a.second or hd >= 2:
                    dve.wait_ge(p_made, u - 1)
                settle(dve)
                for t in range(T):
                    last = dve.tensor_tensor_reduce(z[i][:, t, :], e_ps[i][:, t * P:(t + 1) * P], w[i][:, t, :], -1.0, FAR,
                                                    ALU.add, ALU.min, nmax[i][:, t:t + 1])
                last.then_inc(z_made, 1)
                other()

            def split_sd(a):
                split.start(a.q)
                dve.wait_ge(h_made, a.q + 1)
                if a.third:
                    dve.wait_ge(rows_done, a.q - 1)
                place = cols[a.par][:].rearrange("p (s r) -> p s r", s=2)[:, :, 0:SIDE].rearrange(
                    "p s (t h w) -> p s t h w", t=T, h=H)
                part = [[place[:, side, :, :, i] for side in range(2)] for i in range(3)]
                sd = [h[a.par][:, :, P + side * H:P + (side + 1) * H] for side in range(2)]
                rest = [[sd_rest[:, i, side, :].rearrange("p (t h) -> p t h", t=T) for side in range(2)] for i in range(2)]
                dve.tensor_copy(part[0][0], sd[0])
                split.mark(dve.tensor_copy(part[0][1], sd[1]))
                yield
                split.wait()
                tt(rest[0][0], sd[0], part[0][0], ALU.subtract)
                split.mark(tt(rest[0][1], sd[1], part[0][1], ALU.subtract))
                yield
                split.wait()
                dve.tensor_copy(part[1][0], rest[0][0])
                split.mark(dve.tensor_copy(part[1][1], rest[0][1]))
                yield
                split.wait()
                tt(rest[1][0], rest[0][0], part[1][0], ALU.subtract)
                split.mark(tt(rest[1][1], rest[0][1], part[1][1], ALU.subtract))
                yield
                split.wait()
                dve.tensor_copy(part[2][0], rest[1][0])
                dve.tensor_copy(part[2][1], rest[1][1]).then_inc(cols_made, 1)
                split.end()

            def step(k, c):
                n, f, b, v, r, m = (At(k, c + i) for i in (1, 0, -2, -3, -4, -5))
                sides = []

                def other():
                    while sides:
                        chain = sides.pop(0)
                        if next(chain, "end") != "end":
                            sides.append(chain)
                            return

                def drain():
                    while sides:
                        other()

                def row():
                    if r.real:
                        if r.third:
                            dve.wait_ge(scattered[r.par], 16 * T * r.half)
                            settle(dve)
                        dve.tensor_copy(R[r.par][:, :, 0:P], xg(x_all, r))

                score_unit(k, c, 0, row if n.real else lambda: None)
                if v.real:
                    dve.wait_ge(x2_made, v.q + 1)
                    if v.third:
                        dve.wait_ge(row_made, v.q - 1)
                    settle(dve)
                    for _ in bn(bn2, graph_x(v), c_ln2):
                        pass
                    aggregate(mv2[v.par], bn2, c_ln2, v.q + 1).then_inc(ln2_made, 1)

                if r.real:
                    sides.append(logits(r))
                if m.real:
                    sides.append(find_slots(m, r))
                for _ in range(6):
                    other()
                if b.real:
                    dve.wait_ge(p_made, H * (b.q + 1))
                    dve.reciprocal(rden[:], den[b.par][:]).then_inc(c_norm, 1)
                other()
                score_unit(k, c, 1, other)
                drain()

                if not n.real:
                    row()
                if r.real:
                    sides.append(route(r))
                if n.real:
                    dve.wait_ge(x_in[n.par], 16 * (n.half + 1))
                    if n.second:
                        dve.wait_ge(xn_made, n.q)
                    settle(dve)
                    for _ in bn(bn1, graph_x(n), c_ln1):
                        other()
                    aggregate(mv1, bn1, c_ln1, n.q + 1).then_inc(ln1_made, 1)
                    if not n.second:
                        split_b2()
                        dve.wait_ge(wu_ps, 1)
                        dve.tensor_copy(wu[:, P:HW], seven[:, 0:2 * H]).then_inc(wu_made, 1)
                other()
                score_unit(k, c, 2, other)
                if f.real:
                    for _ in split_sd(f):
                        other()

                if b.real:
                    dve.wait_ge(c_norm, b.q + 1)
                    dve.wait_ge(out_done, b.q + 1)
                    if b.second:
                        dve.wait_ge(x2_made, b.q)
                    tt(outn[:].rearrange("p t (h n) -> p t h n", h=H),
                       seven[:].rearrange("p (t h n) -> p t h n", t=T, h=H),
                       rden[:].rearrange("p h t -> p t h").unsqueeze(3).broadcast_to([P, T, H, HD]),
                       ALU.mult).then_inc(outn_made, 1)
                other()
                if f.real:
                    dve.wait_ge(rows_done, f.q + 1)
                    if f.third:
                        dve.wait_ge(e_done, H * (f.q - 1))
                    dve.tensor_copy(rows[f.par][:].rearrange("p s t n -> p (s t n)"), five[:].bitcast(bf16)).then_inc(rows_made, 1)
                other()
                score_unit(k, c, 3, other)
                drain()

            def logits(r):
                gate.start(r.q)
                if not r.second:
                    dve.wait_ge(gate_in, 32)
                dve.wait_ge(gate_done, r.q + 1)
                tt(lg[:], seven[:, 0:T * E].rearrange("p (t e) -> p t e", t=T),
                   gbias[:].unsqueeze(1).broadcast_to([P, T, E]), ALU.add).then_inc(lg_made, 1)
                yield
                dve.wait_ge(lg_made, r.q + 1)
                gate.mark(dve.reduce_max(lmax[:], lg[:], X))
                yield
                gate.wait()
                gate.end()
                tt(lsh[:], lg[:], lmax[:].unsqueeze(2).broadcast_to([P, T, E]), ALU.subtract).then_inc(lsh_made, 1)

            def route(r):
                topc.start(r.q)
                over = lambda v: v.unsqueeze(2).broadcast_to([P, T, E])
                dve.wait_ge(ex_made, r.q + 1)
                R_ = R[r.par]
                topc.mark(dve.reduce_sum(esum[:, 0, :], ex[:], X))
                yield
                topc.wait()
                topc.mark(dve.reciprocal(esum[:, 1, :], esum[:, 0, :]))
                yield
                topc.wait()
                topc.mark(tt(prob[:], ex[:], over(esum[:, 1, :]), ALU.mult))
                yield
                topc.wait()
                for src, dst in ((prob, top[:, 0]), (left, top[:, 1])):
                    topc.mark(dve.reduce_max(best[:], src[:], X))
                    yield
                    topc.wait()
                    topc.mark(tt(tie[:, 0], src[:], over(best[:]), ALU.is_equal))
                    yield
                    topc.wait()
                    topc.mark(tt(tie[:, 1], tie[:, 0], descend[:], ALU.mult))
                    yield
                    topc.wait()
                    topc.mark(dve.reduce_max(best[:], tie[:, 1], X))
                    yield
                    topc.wait()
                    topc.mark(tt(dst, tie[:, 1], over(best[:]), ALU.is_equal))
                    yield
                    topc.wait()
                    if src is prob:
                        topc.mark(stt(left[:], top[:, 0], -4.0, prob[:], ALU.mult, ALU.add))
                        yield
                        topc.wait()
                topc.mark(tt(top[:, 2], top[:, 0], top[:, 1], ALU.add))
                ts(R_[:, :, ID], R_[:, :, ID], float(2 * T * P), None, ALU.add)
                yield
                topc.wait()
                topc.end()
                if r.second:
                    dve.wait_ge(rank_read, r.q)
                at = 0
                for i in range(E - 1):
                    n = E - 1 - i
                    last = tt(member[:, :, at:at + n], top[:, 2, :, i:i + 1].broadcast_to([P, T, n]),
                              top[:, 2, :, i + 1:E], ALU.mult)
                    at += n
                last.then_inc(member_made, 1)
                yield
                tt(R_[:, :, CW:CW + E], prob[:], top[:, 2], ALU.mult)
                dve.wait_ge(xn2_made, r.q + 1)
                dve.tensor_copy(R_[:, :, RS], rs2[r.par][:])
                dve.tensor_copy(R_[:, :, MEAN], mv2[r.par][:, :, 0]).then_inc(row_made, 1)

            def find_slots(m, r):
                slots.start(m.q)
                dve.wait_ge(rank_done, m.q + 1)
                if r.real:
                    dve.wait_ge(gate_done, r.q + 1)
                ahead = seven[:, AHEAD:TOTAL].rearrange("p (t g) -> p t g", t=T)
                total = seven[:, TOTAL:TOTAL + T * PAIRS].rearrange("p (t g) -> p t g", t=T)
                for t in range(T):
                    slots.mark(tt(run[:, t + 1, :], run[:, t, :], total[:, t, :], ALU.add))
                    yield
                    slots.wait()
                slots.mark(tt(rank[:, 0], run[:, 0:T, :], ahead, ALU.add))
                yield
                slots.wait()
                dve.tensor_copy(run[:, 0, :], run[:, T, :]).then_inc(rank_read, 1)
                slots.mark(tt(rank[:, 1], rank[:, 0], member[:], ALU.mult))
                yield
                slots.wait()
                slots.mark(dve.reduce_sum(slot[:], rank[:, 1], X))
                yield
                slots.wait()
                slots.end()
                dve.tensor_copy(slot_i[m.par][:], slot[:]).then_inc(slot_made, 1)

            steps(dve, step)

            tc = Chain(dve, c_tiles, 15)
            tc.start(0)
            dve.wait_ge(slot_made, GROUPS)
            count, cum, start, n_, lt_end, lt_start, mine, at0, one, final, full = (tiles[:, i, :] for i in (*range(9), 11, 12))
            dve.wait_ge(expert_in, 16 * 4)
            tc.link(tt(count, run[:, 0, :], base[:], ALU.subtract))
            ts(final, count, -float(P), 0.0, ALU.add, ALU.max)
            tc.link(ts(full, count, float(P - 1), None, ALU.add))
            tc.link(dve.tensor_copy(tiles_i[:, 0, :], full))
            tc.link(ts(tiles_i[:, 1, :], tiles_i[:, 0, :], P.bit_length() - 1, None, ALU.arith_shift_right))
            tc.link(dve.tensor_copy(n_, tiles_i[:, 1, :]))
            tc.link(dve.memset(one, 1.0))
            tc.link(dve.tensor_tensor_scan(cum, one, n_, 0.0, ALU.mult, ALU.add))
            tc.link(tt(start, cum, n_, ALU.subtract))
            ts(lt_end, cum, number[:], None, ALU.is_le)
            tc.link(ts(lt_start, start, number[:], None, ALU.is_le))
            ts(at0, start, number[:], -float(P), ALU.subtract, ALU.mult)
            tc.link(tt(mine, lt_start, lt_end, ALU.subtract))
            tt(tiles[:, 13, :], at0, final, ALU.subtract)
            tc.link(tt(at0, at0, final, ALU.min))
            tc.link(stt(at0, at0, -float(DUMMY), base[:], ALU.add, ALU.add))
            tt(tiles[:, 9, :], pair_code[:], mine, ALU.mult)
            tc.link(tt(tiles[:, 10, :], at0, mine, ALU.mult))
            tc.link(dve.reduce_sum(table[:], tiles[:, 9:11, :], X))
            ts(table[:, 1:2], table[:, 1:2], float(DUMMY), None, ALU.add)
            tc.link(stt(tiles[:, 14, :], tiles[:, 13, :], 0.0, mine, ALU.max, ALU.mult))
            dve.reduce_sum(again[:], tiles[:, 14, :], X).then_inc(again_made, 1)
            tc.end()
            dve.wait_ge(table_done, 1)
            dve.tensor_copy(table_i[:], seven[0:2, 0:P]).then_inc(starts_made, 1)
            ts(hide[:], six[:, 0:P], number[:], -float(LEAD), ALU.subtract, ALU.add)
            word = seven[0:1, 0:P].rearrange("r (k j) -> r k j", j=WORD)
            pack = Chain(dve, c_pack, WORD)
            pack.start(0)
            pack.link(dve.tensor_copy(packed[:], word[:, :, WORD - 1]))
            for j in range(WORD - 2, -1, -1):
                pack.link(stt(packed[:], packed[:], float(E * E), word[:, :, j], ALU.mult, ALU.add))
            pack.end()
            dve.tensor_copy(packed_i[:], packed[:]).then_inc(table_made, 1)
            dve.wait_ge(table_made, 1)
            ts(hide[:], hide[:], 0.0, NOWHERE, ALU.is_gt, ALU.mult).then_inc(table_made, 1)
            dve.wait_ge(table_made, 1)
            dve.wait_ge(b2_placed, 16 * 3 * E)

            def stage_expert(k, j, x_, expert):
                a = Tile(k, j)
                if not a.real:
                    return
                dve.tensor_copy(WS[j % 4][x_][:], experts[:, bass.ds(expert, 1), :].rearrange("p a n -> p (a n)")).then_inc(staged, 1)

            def prepare(k, j):
                a = Tile(k, j)
                if not a.real:
                    return
                dve.wait_ge(row_in[a.slot], 16 * (a.turn + 1))
                if a.after(4):
                    dve.wait_ge(xT_done, a.n - 3)
                row = XR[a.slot]
                ts(XN[j % 4][:], row[:, 0:P], row[:, MEAN:MEAN + 1], row[:, RS:RS + 1],
                   ALU.subtract, ALU.mult).then_inc(xn_m, 1)

            def pick_weights(k, j, both):
                a = Tile(k, j)
                if not a.real:
                    return
                for x_, expert in enumerate(both):
                    last = dve.tensor_copy(CS[j % 4][:, x_:x_ + 1], XR[a.slot][:, CW:CW + E][:, bass.ds(expert, 1)])
                last.then_inc(picked, 1)

            def combine(k, j, x_):
                a = Tile(k, j)
                u = a.unit(x_)
                dve.wait_ge(down_done, u + 1)
                if x_ == 0:
                    dve.wait_ge(picked, a.n + 1)
                else:
                    if a.after(TURN):
                        dve.wait_ge(y_out[a.slot], 16 * a.turn)
                    dve.wait_ge(combined, u)
                stt((acc[j % 2], Y[a.slot])[x_][:], down_ps[(2 * j + x_) % 4][:, 0:P], CS[j % 4][:, x_:x_ + 1],
                    (XR[a.slot][:, 0:P], acc[j % 2][:])[x_], ALU.mult, ALU.add).then_inc(combined, 1)

            def load_experts(word):
                experts_of = dve.value_load(packed_i[0:1, bass.ds(word, 1)], min_val=0, max_val=2 ** (6 * WORD) - 1)
                return [[(experts_of >> (6 * j + 3)) & 7, (experts_of >> (6 * j)) & 7] for j in range(WORD)]

            chosen = []

            def tile(k, j):
                if j % WORD == 0:
                    chosen[:] = load_experts(k * (TURN // WORD) + j // WORD + 1)
                both = chosen[j % WORD]
                stage_expert(k, j + LEAD, 0, both[0])
                combine(k, j, 0)
                prepare(k, j + PREPARE)
                pick_weights(k, j + LEAD, both)
                stage_expert(k, j + LEAD, 1, both[1])
                combine(k, j, 1)

            early = load_experts(0)[WORD - LEAD:]
            for j in range(LEAD):
                for x_ in range(2):
                    stage_expert(0, j, x_, early[j][x_])
            for j in range(PREPARE):
                prepare(0, j)
                if j < LEAD:
                    pick_weights(0, j, early[j])
            turns(dve, tile)


_OUTS = [((64 * 128, 128), 'float32')]


def kernel(x, adj, L0_gnn_W, L0_gnn_att_src, L0_gnn_att_dst, L0_ffn_gate_w, L0_ffn_gate_b, L0_ffn_W1, L0_ffn_b1,
           L0_ffn_W2, L0_ffn_b2):
    import numpy as np
    import concourse.bacc as _bacc
    from concourse import mybir as _mybir
    from concourse.bass_utils import run_bass_kernel_spmd as _run

    G, P, E, F, H = 64, 128, 8, 256, 4
    ready = np.ascontiguousarray
    W = np.asarray(L0_gnn_W)
    ins = {
        "x": ready(np.asarray(x).transpose(1, 0, 2)),
        "adj": ready(np.asarray(adj).transpose(1, 0, 2)),
        "w_rows": ready(W),
        "w_cols": ready(W.T),
        "att_cols": ready(np.stack([np.asarray(L0_gnn_att_src).reshape(P), np.asarray(L0_gnn_att_dst).reshape(P)], axis=1)),
        "gate_w": ready(L0_ffn_gate_w),
        "gate_b": ready(L0_ffn_gate_b),
        "w1": ready(np.asarray(L0_ffn_W1).transpose(1, 0, 2)),
        "b1": ready(np.asarray(L0_ffn_b1).reshape(E, F // P, P).transpose(2, 0, 1)),
        "w2": ready(np.asarray(L0_ffn_W2).reshape(E, F // P, P, P).transpose(2, 0, 1, 3).reshape(P, E, F)),
        "b2": ready(np.asarray(L0_ffn_b2).reshape(E * P)),
        "pairs": np.array([E * a + b for a in range(E) for b in range(a + 1, E)], np.float32),
    }
    nc = _bacc.Bacc("TRN2", target_bir_lowering=False, num_devices=1)
    args = [nc.dram_tensor(f"in_{n}", a.shape, _mybir.dt.from_np(a.dtype), kind="ExternalInput").ap()
            for n, a in ins.items()]
    for i, (shape, dtype) in enumerate(_OUTS):
        dt = _mybir.dt.from_np(np.dtype(dtype))
        args.append(nc.dram_tensor(f"out_{i}", shape, dt, kind="ExternalOutput").ap())
    bass_gat_moe_kernel(nc, *args)
    r = _run(nc, [{f"in_{n}": a for n, a in ins.items()}], core_ids=[0])
    return r.results[0]["out_0"].reshape(G, P, P)
```
